# Optimizing a Trainium2 kernel written in Bass

```python
import numpy as np
import jax
import jax.numpy as jnp

def _softmax(x, axis=-1):
    return jax.nn.softmax(x, axis=axis)

def _gelu(x):
    return jax.nn.gelu(x, approximate=True)

def _silu(x):
    return jax.nn.silu(x)

def _sigmoid(x):
    return jax.nn.sigmoid(x)

def _layernorm(x, axis=-1, eps=1e-05):
    m = jnp.mean(x, axis=axis, keepdims=True)
    v = jnp.var(x, axis=axis, keepdims=True)
    return (x - m) / jnp.sqrt(v + eps)

def _scatter_add(tgt, idx, src, axis=0):
    return tgt.at[idx].add(src)

def _segment_sum(src, seg, n):
    return jax.ops.segment_sum(src, seg, n)
kernel_name = 'mk_vit_tower_d1_tok_img768_r4_b39f22'

def setup_inputs(seed: int=0):
    np.random.seed(seed)
    _w = jnp.asarray

    def _rec_inputs():
        import jax
        import jax.numpy as jnp
        _rk = jax.random.key(seed)
        x = -0.000222058 + 0.999998 * jax.random.normal(jax.random.fold_in(_rk, 1), (64, 3, 96, 96), jnp.float32)
        return x
    x = _rec_inputs()

    def _L0_tok_setup():
        import jax, jax.numpy as jnp
        import numpy as np
        PATCH = 16

        def _patchify(x, patch):
            b, c, H, W = x.shape
            ph_pad, pw_pad = (H % patch, W % patch)
            x = jnp.pad(x, ((0, 0), (0, 0), (ph_pad, 0), (pw_pad, 0)))
            H2, W2 = (H + ph_pad, W + pw_pad)
            nh, nw = (H2 // patch, W2 // patch)
            x = x.reshape(b, c, nh, patch, nw, patch)
            x = x.transpose(0, 2, 4, 3, 5, 1)
            return x.reshape(b, nh * nw, patch * patch * c)
        key = jax.random.key(seed)
        k1, k2, k3 = jax.random.split(key, 3)
        d_model, c = (192, 3)
        in_feat = PATCH * PATCH * c
        x = jax.random.normal(k1, (32, c, 128, 128), dtype=jnp.float32)
        W = jax.random.normal(k2, (d_model, in_feat), dtype=jnp.float32) * (1.0 / np.sqrt(in_feat))
        b = jax.random.normal(k3, (d_model,), dtype=jnp.float32) * 0.01
        return {'x': x, 'W': W, 'b': b}
    _L0_tok_all = _L0_tok_setup()
    _L0_tok_in = {k: v for k, v in _L0_tok_all.items() if k in ('W', 'b')}
    del _L0_tok_all

    def _L0_attn_setup():
        import jax, jax.numpy as jnp
        import numpy as np
        B, N, E, H = (2, 512, 192, 12)
        D = E // H
        G = 16
        LN_EPS = 1e-05

        def _layernorm(x, w, b):
            mu = jnp.mean(x, axis=-1, keepdims=True)
            var = jnp.mean(jnp.square(x - mu), axis=-1, keepdims=True)
            return (x - mu) * jax.lax.rsqrt(var + LN_EPS) * w + b
        key = jax.random.key(seed)
        ks = jax.random.split(key, 8)
        s = E ** (-0.5)
        x = jax.random.normal(ks[0], (B, N, E), jnp.float32)
        log_slope = -2.0 ** (-8.0 * (jnp.arange(H, dtype=jnp.float32) + 1.0) / H)
        Wq = jax.random.normal(ks[1], (E, E), jnp.float32) * s
        Wk = jax.random.normal(ks[2], (E, E), jnp.float32) * s
        Wv = jax.random.normal(ks[3], (E, E), jnp.float32) * s
        Wo = jax.random.normal(ks[4], (E, E), jnp.float32) * s
        Wg1 = jax.random.normal(ks[5], (E, G), jnp.float32) * s
        Wg2 = jax.random.normal(ks[6], (G, E), jnp.float32) * G ** (-0.5)
        ln_w = jnp.ones((E,), jnp.float32)
        ln_b = jnp.zeros((E,), jnp.float32)
        return {'x': x, 'log_slope': log_slope, 'Wq': Wq, 'Wk': Wk, 'Wv': Wv, 'Wo': Wo, 'Wg1': Wg1, 'Wg2': Wg2, 'ln_w': ln_w, 'ln_b': ln_b}
    _L0_attn_all = _L0_attn_setup()
    _L0_attn_in = {k: v for k, v in _L0_attn_all.items() if k in ('log_slope', 'Wq', 'Wk', 'Wv', 'Wo', 'Wg1', 'Wg2', 'ln_w', 'ln_b')}
    del _L0_attn_all

    def _L0_ffn_setup():
        import jax, jax.numpy as jnp
        import numpy as np
        import math
        B, S, D = (4, 1024, 192)
        E = 8
        TOP_K = 2
        H = 512
        CAP_F = 1.25
        EPS = 1e-06
        ALPHA = 1.0
        key = jax.random.key(seed)
        k0, k1, k2, k3 = jax.random.split(key, 4)
        x = jax.random.normal(k0, (B, S, D), jnp.float32)
        gate_w = jax.random.normal(k1, (E, D), jnp.float32) * 0.02
        w13 = jax.random.normal(k2, (E, 2 * H, D), jnp.float32) * 0.02
        w2 = jax.random.normal(k3, (E, D, H), jnp.float32) * 0.02
        norm_w = jnp.ones((E, D), jnp.float32)
        return {'x': x, 'gate_w': gate_w, 'w13': w13, 'w2': w2, 'norm_w': norm_w}
    _L0_ffn_all = _L0_ffn_setup()
    _L0_ffn_in = {k: v for k, v in _L0_ffn_all.items() if k in ('gate_w', 'w13', 'w2', 'norm_w')}
    del _L0_ffn_all
    return {'x': x, 'L0_tok_W': _L0_tok_in['W'], 'L0_tok_b': _L0_tok_in['b'], 'L0_attn_log_slope': _L0_attn_in['log_slope'], 'L0_attn_Wq': _L0_attn_in['Wq'], 'L0_attn_Wk': _L0_attn_in['Wk'], 'L0_attn_Wv': _L0_attn_in['Wv'], 'L0_attn_Wo': _L0_attn_in['Wo'], 'L0_attn_Wg1': _L0_attn_in['Wg1'], 'L0_attn_Wg2': _L0_attn_in['Wg2'], 'L0_attn_ln_w': _L0_attn_in['ln_w'], 'L0_attn_ln_b': _L0_attn_in['ln_b'], 'L0_ffn_gate_w': _L0_ffn_in['gate_w'], 'L0_ffn_w13': _L0_ffn_in['w13'], 'L0_ffn_w2': _L0_ffn_in['w2'], 'L0_ffn_norm_w': _L0_ffn_in['norm_w']}

def reference(x, L0_tok_W, L0_tok_b, L0_attn_log_slope, L0_attn_Wq, L0_attn_Wk, L0_attn_Wv, L0_attn_Wo, L0_attn_Wg1, L0_attn_Wg2, L0_attn_ln_w, L0_attn_ln_b, L0_ffn_gate_w, L0_ffn_w13, L0_ffn_w2, L0_ffn_norm_w):
    import jax
    import jax.numpy as jnp

    def _L0_tok_ref(x, W, b):
        import jax, jax.numpy as jnp
        import numpy as np
        PATCH = 16

        def _patchify(x, patch):
            b, c, H, W = x.shape
            ph_pad, pw_pad = (H % patch, W % patch)
            x = jnp.pad(x, ((0, 0), (0, 0), (ph_pad, 0), (pw_pad, 0)))
            H2, W2 = (H + ph_pad, W + pw_pad)
            nh, nw = (H2 // patch, W2 // patch)
            x = x.reshape(b, c, nh, patch, nw, patch)
            x = x.transpose(0, 2, 4, 3, 5, 1)
            return x.reshape(b, nh * nw, patch * patch * c)
        patches = _patchify(x, PATCH)
        return jnp.einsum('bnf,df->bnd', patches, W) + b

    def _L0_attn_ref(x, log_slope, Wq, Wk, Wv, Wo, Wg1, Wg2, ln_w, ln_b):
        import jax, jax.numpy as jnp
        import numpy as np
        B, N, E, H = (2, 512, 192, 12)
        D = E // H
        G = 16
        LN_EPS = 1e-05

        def _layernorm(x, w, b):
            mu = jnp.mean(x, axis=-1, keepdims=True)
            var = jnp.mean(jnp.square(x - mu), axis=-1, keepdims=True)
            return (x - mu) * jax.lax.rsqrt(var + LN_EPS) * w + b
        b, n, e = x.shape
        h = log_slope.shape[0]
        d = e // h
        silu = jax.nn.silu
        q = silu(x @ Wq).reshape(b, n, h, d).transpose(0, 2, 1, 3)
        k = silu(x @ Wk).reshape(b, n, h, d).transpose(0, 2, 1, 3)
        v = silu(x @ Wv).reshape(b, n, h, d).transpose(0, 2, 1, 3)
        idx = jnp.arange(n, dtype=jnp.float32)
        diff = idx[:, None] - idx[None, :]
        keep = diff >= 0
        decay = jnp.where(keep, jnp.exp(log_slope[:, None, None] * jnp.maximum(diff, 0.0)), 0.0)
        energy = jnp.einsum('bhnd,bhmd->bhnm', q, k) * decay
        out = jnp.einsum('bhnm,bhmd->bhnd', energy, v)
        out = out.transpose(0, 2, 1, 3).reshape(b, n, e)
        gate = jax.nn.sigmoid(x @ Wg1 @ Wg2)
        out = out * gate
        out = out @ Wo
        out = _layernorm(out, ln_w, ln_b)
        return out

    def _L0_ffn_ref(x, gate_w, w13, w2, norm_w):
        import jax, jax.numpy as jnp
        import numpy as np
        import math
        B, S, D = (4, 1024, 192)
        E = 8
        TOP_K = 2
        H = 512
        CAP_F = 1.25
        EPS = 1e-06
        ALPHA = 1.0
        Bx, Sx, Dx = x.shape
        N = Bx * Sx
        cap = int(math.ceil(CAP_F * TOP_K * N / E))
        xf = x.reshape(N, Dx)
        logits = xf.astype(jnp.float32) @ gate_w.T
        probs = jax.nn.softmax(logits, axis=-1)
        top_p, top_i = jax.lax.top_k(probs, TOP_K)
        w = top_p / jnp.sum(top_p, axis=-1, keepdims=True)
        flat_e = top_i.reshape(-1)
        onehot = jax.nn.one_hot(flat_e, E, dtype=jnp.int32)
        pos = jnp.take_along_axis(jnp.cumsum(onehot, axis=0) - 1, flat_e[:, None], axis=1)[:, 0]
        keep = pos < cap
        didx = flat_e * cap + jnp.minimum(pos, cap - 1)
        safe = jnp.where(keep, didx, E * cap)
        x_rep = jnp.repeat(xf, TOP_K, axis=0)
        buf = jnp.zeros((E * cap + 1, Dx), x.dtype).at[safe].set(x_rep)
        buf = buf[:-1].reshape(E, cap, Dx)
        z = 2.0 * buf
        z = z * jax.lax.rsqrt(jnp.mean(z * z, axis=-1, keepdims=True) + EPS)
        z = z * norm_w[:, None, :]
        gu = jnp.einsum('ecd,ehd->ech', z, w13)
        g, u = jnp.split(gu, 2, axis=-1)
        y = buf + ALPHA * jnp.einsum('ech,edh->ecd', jax.nn.silu(g) * u, w2)
        y_tok = y.reshape(E * cap, Dx)[didx]
        cw = (w.reshape(-1) * keep.astype(w.dtype)).astype(x.dtype)
        out = (cw[:, None] * y_tok).reshape(N, TOP_K, Dx).sum(axis=1)
        return out.reshape(Bx, Sx, Dx)
    h = _L0_tok_ref(x, L0_tok_W, L0_tok_b)
    h = h + _L0_attn_ref(_layernorm(h, axis=-1), L0_attn_log_slope, L0_attn_Wq, L0_attn_Wk, L0_attn_Wv, L0_attn_Wo, L0_attn_Wg1, L0_attn_Wg2, L0_attn_ln_w, L0_attn_ln_b)
    h = h + _L0_ffn_ref(_layernorm(h, axis=-1), L0_ffn_gate_w, L0_ffn_w13, L0_ffn_w2, L0_ffn_norm_w)
    return h

_drawn_inputs = setup_inputs


def setup_inputs(seed=0):
    import zlib

    import numpy as np

    out = dict(_drawn_inputs(seed))
    spreads = {'L0_attn_ln_w': (1.0, 0.2), 'L0_attn_ln_b': (0.0, 0.1), 'L0_ffn_norm_w': (1.0, 0.6)}
    factors = {'L0_ffn_w13': 8.0, 'L0_ffn_w2': 8.0}
    for name, (base, spread) in spreads.items():
        noise = np.random.default_rng([zlib.crc32(name.encode()), seed]).standard_normal(out[name].shape)
        drawn = base * np.exp(spread * noise) if base else spread * noise
        out[name] = jnp.asarray(drawn.astype(out[name].dtype))
    for name, factor in factors.items():
        out[name] = (out[name] * factor).astype(out[name].dtype)
    return out
```

```python
from contextlib import ExitStack

import numpy as np
import concourse.bass as bass
from concourse import mybir

F32 = mybir.dt.float32
F32R = mybir.dt.float32r
BF16 = mybir.dt.bfloat16
I32 = mybir.dt.int32
ALU = mybir.AluOpType
ACT = mybir.ActivationFunctionType
AX_X = mybir.AxisListType.X

P = 128
B_IMG, CH_IN, IMG, PATCH = 64, 3, 96, 16
GRID = IMG // PATCH
SEQ = GRID * GRID
NTOK = B_IMG * SEQ
FEAT = PATCH * PATCH * CH_IN
KC = FEAT // P
D = 192
HALF = D // 2
NT = NTOK // P
RING = 3
ROUNDS = NT // RING
HEADS = 12
HD = D // HEADS
G = 16
BLK = 2 * SEQ
CB = 4
CHUNK = CB * BLK
NCHUNK = NTOK // CHUNK
PAIRS = 3
E = 8
HID = 512
HC = HID // P
CAP = 720
SP_ = 120
SJ = CAP // SP_
MOV = CAP // 2
ROW = E + D
TAIL = D - P
TROW = ROW + TAIL
EPS_LN = 1e-5
EPS_FFN = 1e-6
FAR = 1000.0

_C = {}
_at = 0
for _name, _n in (("ident", P), ("tri", P), ("mask", 2), ("diff", BLK), ("keep", BLK), ("slot_p", SP_),
                  ("slot_ej", E * SJ), ("slot_id", E * SJ), ("expert", E), ("rank", E), ("reset", E * NT),
                  ("tile1", NT), ("part", 1)):
    _C[_name] = slice(_at, _at + _n)
    _at += _n
NCONST = _at


def constants():
    c = np.zeros((P, NCONST), np.float32)
    p = np.arange(P)
    c[:, _C["ident"]] = np.eye(P)
    c[:, _C["tri"]] = p[:, None] < p[None, :]
    c[:, _C["mask"]] = np.stack([p % 32 < 16, p % 32 >= 16], 1)
    m, n = np.arange(BLK)[:, None], np.arange(BLK)[None, :]
    keep = (n >= m) & (n // SEQ == m // SEQ)
    c[:BLK, _C["diff"]] = (n - m) * keep
    c[:BLK, _C["keep"]] = keep
    c[:, _C["slot_p"]] = np.arange(SP_)
    c[:, _C["slot_ej"]] = np.arange(E * SJ)
    c[:, _C["slot_id"]] = NTOK + P + p[:, None] + SP_ * (np.arange(E * SJ) % SJ)[None, :]
    c[:, _C["expert"]] = np.arange(E)
    c[:, _C["rank"]] = E - np.arange(E)
    c[:, _C["reset"]] = (np.arange(E * NT) % NT) > 0
    c[:, _C["tile1"]] = np.arange(NT) + 1
    c[:, _C["part"]] = p[:, None]
    return c


def build(nc, xT, wT, b, ls, wq, wkg, wv, wg2, wo, lnw, lnb, gwT, w13T, w2T, nwT, const, out):
    table = nc.dram_tensor("table", [NTOK, TROW], F32).ap()
    with ExitStack() as ctx:
        def sb(name, shape, dt=F32):
            return ctx.enter_context(nc.sbuf_tensor(name, shape, dt))

        def sem(name):
            return ctx.enter_context(nc.semaphore(name))

        def need(eng, s, value):
            if not (isinstance(value, int) and value <= 0):
                eng.wait_ge(s, value)

        cst = sb("cst", [P, NCONST])
        wT_s = sb("wT_s", [P, KC, D])
        b_s = sb("b_s", [P, D])
        ls_s = sb("ls_s", [BLK, HEADS])
        wq_s = sb("wq_s", [HALF, 2, D])
        wkg_s = sb("wkg_s", [HALF, 2, D + G])
        wv_s = sb("wv_s", [HALF, 2, D])
        wg2_s = sb("wg2_s", [HALF + G, D])
        wo_s = sb("wo_s", [HALF, 2, D])
        wo_h = sb("wo_h", [HALF, 2, D])
        lnw_s = sb("lnw_s", [P, D])
        lnb_s = sb("lnb_s", [P, D])
        gw_s = sb("gw_s", [HALF, 2, E])
        nwA = sb("nwA", [P, E])
        nwB = sb("nwB", [P, E])
        ones = sb("ones", [P, P])
        mhalf = sb("mhalf", [P, RING])

        hold0 = sb("hold0", [P, RING * KC * P])
        xt = [hold0[:, u * KC * P:(u + 1) * KC * P].rearrange("p (k n) -> p k n", k=KC) for u in range(RING)]
        h = sb("h", [P, NT, D])
        xn = [sb(f"xn{u}", [P, D]) for u in range(RING)]
        st = [sb(f"st{u}", [P, 6]) for u in range(RING)]
        mv = sb("mv", [P, RING, 2])
        ve = sb("ve", [P, RING])
        rstd = sb("rstd", [P, RING])
        hold1 = sb("hold1", [P, 2 * NTOK])
        hold2 = sb("hold2", [P, 2 * NTOK])
        xnT = hold1[0:HALF, :].rearrange("p (f n) -> p f n", f=2)
        goT = hold2[0:HALF, :].rearrange("p (f n) -> p f n", f=2)

        decay = sb("decay", [BLK, HEADS, BLK])
        xs = [sb(f"xs{w}", [HALF, 2, CHUNK]) for w in range(2)]
        qm = [[sb(f"qm{w}{f}", [HALF, 2, CHUNK]) for f in range(2)] for w in range(2)]
        kT = [[sb(f"kT{w}{f}", [HALF, CHUNK]) for f in range(2)] for w in range(2)]
        g1 = [sb(f"g1{w}", [HALF + G, CHUNK]) for w in range(2)]
        gate = [sb(f"gate{w}", [HALF, 2, CHUNK]) for w in range(2)]
        vp = [sb(f"vp{w}", [BLK, 2 * PAIRS, 4 * HD]) for w in range(2)]
        ed = [sb(f"ed{w}", [BLK, 2, PAIRS, 2 * BLK]) for w in range(2)]

        gos = [sb(f"gos{u}", [HALF, 2, P]) for u in range(RING)]
        y1 = [sb(f"y1{u}", [P, D]) for u in range(RING)]
        y2 = [sb(f"y2{u}", [P, D]) for u in range(RING)]
        st2 = [sb(f"st2{u}", [P, 6]) for u in range(RING)]
        mv2 = sb("mv2", [P, RING, 2])
        ve2 = sb("ve2", [P, RING])
        rstd2 = sb("rstd2", [P, RING])
        ssq = sb("ssq", [P, RING])
        ve3 = sb("ve3", [P, RING])
        rms = sb("rms", [P, NT])
        xf = [sb(f"xf{u}", [P, D]) for u in range(RING)]
        xfT = [sb(f"xfT{u}", [HALF, 2, P]) for u in range(RING)]
        zrow = sb("zrow", [P, NT, ROW])

        top = sb("top", [P, NT])
        ex = sb("ex", [P, E, NT])
        probs = sb("probs", [P, E, NT])
        left = sb("left", [P, E, NT])
        same = sb("same", [P, E, NT])
        best = sb("best", [P, 2, NT])
        rank = sb("rank", [P, NT])
        hot = sb("hot", [P, 2, E, NT])
        cnt = sb("cnt", [P, E, NT])
        upto = sb("upto", [P, E, NT])
        pick = sb("pick", [P, 2, E, NT])
        pos = sb("pos", [P, 2, NT])
        exp_of = sb("exp_of", [P, 2, NT])
        kept = sb("kept", [P, 2, NT])
        cw = sb("cw", [P, 2, NT])
        cws = sb("cws", [P, NT])
        jj = sb("jj", [P, 2, NT])
        pl = sb("pl", [P, 2, NT])
        ej = sb("ej", [P, 2, NT])
        far = sb("far", [P, 2, NT])
        hot_p = hold2[:, 0:2 * NT * SP_ // 2].bitcast(BF16).rearrange("p (c s) -> p c s", s=SP_)
        at = 2 * NT * SP_ // 2
        hot_e = hold2[:, at:at + 2 * NT * E * SJ].bitcast(BF16).rearrange("p (c x s) -> p c x s", x=2, s=E * SJ)
        tok_of = sb("tok_of", [SP_, 2 * E * SJ])
        token = sb("token", [SP_, E * SJ])
        empty = sb("empty", [SP_, E * SJ])
        gather_at = sb("gather_at", [SP_, E * SJ], I32)
        add_at = sb("add_at", [SP_, E * SJ], I32)

        act_h = hold1[:, 0:HC * CAP].rearrange("p (c n) -> p c n", c=HC)
        silu_g = [hold1[:, HC * CAP + s * MOV:HC * CAP + (s + 1) * MOV] for s in range(2)]
        wA = sb("wA", [P, 2 * HID])
        wB = sb("wB", [P, 2 * HID])
        wA_hi = sb("wA_hi", [P, 2 * HID], F32R)
        wA_lo = sb("wA_lo", [P, 2 * HID], F32R)
        wB_hi = sb("wB_hi", [P, 2 * HID], F32R)
        wB_lo = sb("wB_lo", [TAIL, 2 * HID], F32R)
        w2_s = [sb(f"w2_s{u}", [P, HC, D]) for u in range(2)]
        zin = [sb(f"zin{u}", [SP_, SJ, TROW]) for u in range(2)]
        zA_hi = sb("zA_hi", [P, CAP], F32R)
        zA_lo = sb("zA_lo", [P, CAP], F32R)
        zB = sb("zB", [P, CAP], F32R)
        wslot = [sb(f"wslot{u}", [SP_, SJ]) for u in range(2)]
        yo = [hold0[0:SP_, u * SJ * D:(u + 1) * SJ * D].rearrange("p (j d) -> p j d", j=SJ) for u in range(2)]
        gi = [sb(f"gi{u}", [SP_, SJ], I32) for u in range(2)]
        si = sb("si", [SP_, SJ], I32)

        bank = [ctx.enter_context(nc.psum_tensor(f"bank{i}", [P, 512], F32)) for i in range(5)]
        trio = ctx.enter_context(nc.psum_tensor("trio", [P, 3, 512], F32))
        ps_h = [bank[0], bank[1], bank[2]]
        ps_t = [trio[:, u, :] for u in range(RING)]
        ps_proj = [bank[0], bank[1]]
        ps_v = bank[2]
        ps_o = [bank[3], bank[4]]
        ps_w = [bank[0], bank[1], bank[2]]
        ps_l = bank[3]
        ps_d = bank[4]
        ps_s = bank[0]
        ps_z = [bank[0], bank[1]]
        ps_g = [bank[2], bank[3]]
        ps_u = [bank[4], trio[:, 0, :]]
        ps_y = [trio[:, 1, :], trio[:, 2, :]]

        c_in = sem("c_in")
        w_in = sem("w_in")
        x_in = [sem(f"x_in{u}") for u in range(RING)]
        pads_out = sem("pads_out")
        ones_set = sem("ones_set")
        embed_done = sem("embed_done")
        h_ready = sem("h_ready")
        st_ready = sem("st_ready")
        mv_ready = sem("mv_ready")
        ve_ready = sem("ve_ready")
        rstd_ready = sem("rstd_ready")
        xn_ready = sem("xn_ready")
        xn_turned = sem("xn_turned")
        xnT_ready = sem("xnT_ready")
        exp_ready = sem("exp_ready")
        decay_ready = sem("decay_ready")
        woh_ready = sem("woh_ready")
        vp_zero = sem("vp_zero")
        xs_ready = sem("xs_ready")
        proj_done = sem("proj_done")
        proj_taken = sem("proj_taken")
        act_step = sem("act_step")
        g1_ready = sem("g1_ready")
        v_done = sem("v_done")
        v_ready = sem("v_ready")
        energy_done = sem("energy_done")
        ed_ready = sem("ed_ready")
        av_done = sem("av_done")
        go_ready = sem("go_ready")
        hb_ready = sem("hb_ready")
        gos_ready = sem("gos_ready")
        wo_done = sem("wo_done")
        stw_ready = sem("stw_ready")
        mvw_ready = sem("mvw_ready")
        vew_ready = sem("vew_ready")
        rstdw_ready = sem("rstdw_ready")
        y1_ready = sem("y1_ready")
        y2_ready = sem("y2_ready")
        h2_ready = sem("h2_ready")
        st2_ready = sem("st2_ready")
        mv2_ready = sem("mv2_ready")
        ve2_ready = sem("ve2_ready")
        rstd2_ready = sem("rstd2_ready")
        xf_ready = sem("xf_ready")
        ssq_ready = sem("ssq_ready")
        ve3_ready = sem("ve3_ready")
        rms_ready = sem("rms_ready")
        zn_ready = sem("zn_ready")
        xf_turned = sem("xf_turned")
        xfT_ready = sem("xfT_ready")
        logits_done = sem("logits_done")
        ex_ready = sem("ex_ready")
        probs_exp = sem("probs_exp")
        route_step = sem("route_step")
        counts_ready = sem("counts_ready")
        places_done = sem("places_done")
        hots_ready = sem("hots_ready")
        tokens_done = sem("tokens_done")
        index_ready = sem("index_ready")
        weights_ready = sem("weights_ready")
        base_ready = sem("base_ready")
        table_out = sem("table_out")
        base_out = sem("base_out")
        we_in = [sem(f"we_in{u}") for u in range(2)]
        w2_in = [sem(f"w2_in{u}") for u in range(2)]
        rows_in = [sem(f"rows_in{u}") for u in range(2)]
        gi_ready = sem("gi_ready")
        si_ready = sem("si_ready")
        w_hi = sem("w_hi")
        w_split = sem("w_split")
        z_turned = sem("z_turned")
        z_hi = sem("z_hi")
        z_split = sem("z_split")
        wslot_ready = sem("wslot_ready")
        g_done = sem("g_done")
        u_done = sem("u_done")
        silu_ready = sem("silu_ready")
        a_ready = sem("a_ready")
        ffn_done = sem("ffn_done")
        y_ready = sem("y_ready")
        added = sem("added")

        def apart(eng):
            eng.wait_ge(c_in, 16)

        def half_of(e, u):
            return (e - u) // 2

        def col(name, rows=P):
            return cst[0:rows, _C[name]]

        W_LOADS = 14

        block = ctx.enter_context(nc.Block())

        @block.sync
        def _(sp):
            sp.dma_start(wT_s[:, :, :], wT.rearrange("(k p) d -> p k d", p=P)).then_inc(w_in, 16)

            def load_x(it):
                for u in range(RING):
                    t = RING * it + u
                    need(sp, embed_done, t - RING + 1)
                    sp.dma_start(hold0[:, u * KC * P:(u + 1) * KC * P],
                                 xT[bass.ds(t * P, P), :]).then_inc(x_in[u], 16)

            load_x(0)
            sp.dma_start(cst[:, :], const).then_inc(c_in, 16)
            sp.dma_start(b_s[:, :], b.partition_broadcast(P)).then_inc(w_in, 16)
            sp.dma_start(ls_s[:, :], ls.partition_broadcast(BLK)).then_inc(w_in, 16)
            sp.dma_start(wq_s[:, :, :], wq.rearrange("(f p) d -> p f d", p=HALF)).then_inc(w_in, 16)
            sp.dma_start(wkg_s[:, :, :], wkg.rearrange("(f p) d -> p f d", p=HALF)).then_inc(w_in, 16)
            sp.dma_start(wv_s[:, :, :], wv.rearrange("(f p) d -> p f d", p=HALF)).then_inc(w_in, 16)
            sp.dma_start(wg2_s[HALF:HALF + G, :], wg2).then_inc(w_in, 16)
            sp.dma_start(wo_s[:, :, :], wo.rearrange("(f p) d -> p f d", p=HALF)).then_inc(w_in, 16)
            sp.dma_start(lnw_s[:, :], lnw.partition_broadcast(P)).then_inc(w_in, 16)
            sp.dma_start(lnb_s[:, :], lnb.partition_broadcast(P)).then_inc(w_in, 16)
            sp.dma_start(gw_s[:, :, :], gwT.rearrange("(f p) e -> p f e", p=HALF)).then_inc(w_in, 16)
            sp.dma_start(nwA[:, :], nwT[0:P, :]).then_inc(w_in, 16)
            for f in range(2):
                sp.dma_start(nwB[f * TAIL:(f + 1) * TAIL, :], nwT[P:D, :]).then_inc(w_in, 16)
            with sp.Fori(1, ROUNDS) as it:
                load_x(it)
            sp.wait_ge(ones_set, 3)
            sp.dma_start(out[NTOK:NTOK + CAP, :].rearrange("(p j) d -> p j d", j=SJ),
                         zin[0][:, :, 0:D]).then_inc(pads_out, 16)

            def load_expert(e, u):
                need(sp, w_split, 2 * e)
                sp.dma_start(wA[:, :], w13T[bass.ds(e * D, P), :]).then_inc(we_in[u], 16)
                for f in range(2):
                    sp.dma_start(wB[f * TAIL:(f + 1) * TAIL, :],
                                 w13T[bass.ds(e * D + P, TAIL), :]).then_inc(we_in[u], 16)
                need(sp, ffn_done, SJ * (e - 1))
                sp.dma_start(w2_s[u][:, :, :],
                             w2T[bass.ds(e * HID, HID), :].rearrange("(c p) d -> p c d", p=P)).then_inc(w2_in[u], 16)

            load_expert(0, 0)
            sp.wait_ge(zn_ready, NT)
            table_v = table.rearrange("(t p) d -> p t d", p=P)
            sp.dma_start(table_v[:, :, ROW:TROW], zrow[:, :, E + P:ROW]).then_inc(table_out, 16)
            sp.wait_ge(weights_ready, 1)
            sp.dma_start(table_v[:, :, 0:ROW], zrow[:, :, :]).then_inc(table_out, 16)
            load_expert(1, 1)
            sp.wait_ge(base_ready, NT)
            sp.dma_start(out[0:NTOK, :].rearrange("(t p) d -> p t d", p=P), h[:, :, :]).then_inc(base_out, 16)
            with sp.Fori(1, E // 2) as it:
                load_expert(2 * it, 0)
                load_expert(2 * it + 1, 1)
            sp.wait_ge(pads_out, 16)

        @block.gpsimd
        def _(pool):
            pool.memset(ones[:, :], 1.0).then_inc(ones_set, 1)
            pool.memset(mhalf[:, :], -0.5).then_inc(ones_set, 1)
            pool.memset(zin[0][:, :, :], 0.0).then_inc(ones_set, 1)
            for w in range(2):
                pool.memset(vp[w][:, :, :], 0.0).then_inc(vp_zero, 1)
            pool.wait_ge(ones_set, 3)

            with pool.Fori(0, ROUNDS) as it:
                pool.wait_ge(ve_ready, it + 1)
                pool.tensor_tensor(rstd[:, :], ve[:, :], mhalf[:, :], ALU.pow).then_inc(rstd_ready, 1)

            pool.wait_ge(w_in, 16 * W_LOADS)
            pool.wait_ge(xnT_ready, NT)

            def take_chunk(c, w):
                need(pool, v_done, CB * (c - 1))
                pool.tensor_copy(xs[w][:, :, :], xnT[:, :, bass.ds(c * CHUNK, CHUNK)]).then_inc(xs_ready, 1)

            take_chunk(0, 0)
            take_chunk(1, 1)
            with pool.Fori(1, NCHUNK // 2) as it:
                take_chunk(2 * it, 0)
                take_chunk(2 * it + 1, 1)
            with pool.Fori(0, NT) as t:
                pool.tensor_tensor(h[:, bass.ds(t, 1), :], h[:, bass.ds(t, 1), :], lnb_s[:, :].unsqueeze(1),
                                   ALU.add).then_inc(hb_ready, 1)

            with pool.Fori(0, ROUNDS) as it:
                pool.wait_ge(vew_ready, it + 1)
                pool.tensor_tensor(rstd[:, :], ve[:, :], mhalf[:, :], ALU.pow).then_inc(rstdw_ready, 1)
                for u in range(RING):
                    t = RING * it + u
                    pool.wait_ge(y1_ready, t + 1)
                    pool.tensor_tensor(y2[u][:, :], y1[u][:, :], lnw_s[:, :], ALU.mult).then_inc(y2_ready, 1)
                    pool.wait_ge(y2_ready, t + 1)
                    pool.tensor_tensor(h[:, bass.ds(t, 1), :], h[:, bass.ds(t, 1), :], y2[u][:, :].unsqueeze(1),
                                       ALU.add).then_inc(h2_ready, 1)
                pool.wait_ge(ve2_ready, it + 1)
                pool.tensor_tensor(rstd2[:, :], ve2[:, :], mhalf[:, :], ALU.pow).then_inc(rstd2_ready, 1)
                pool.wait_ge(ve3_ready, it + 1)
                pool.tensor_tensor(rms[:, bass.ds(RING * it, RING)], ve3[:, :], mhalf[:, :],
                                   ALU.pow).then_inc(rms_ready, 1)

            pool.wait_ge(index_ready, 2)

            def gather(e, u):
                need(pool, z_turned, 4 * (e - 1))
                need(pool, wslot_ready, e - 1)
                pool.tensor_copy(gi[u][:, :], gather_at[:, bass.ds(e * SJ, SJ)]).then_inc(gi_ready, 1)
                index_copied = pool.to_reg(e + 1)
                apart(pool)
                pool.wait_ge(gi_ready, index_copied)
                for j in range(SJ):
                    pool.indirect_dma_start(out=zin[u][:, j, :], out_offset=None, in_=table,
                                            in_offset=bass.IndirectOffsetOnAxis(ap=gi[u][:, j:j + 1], axis=0),
                                            bounds_check=NTOK - 1, oob_is_err=True).then_inc(rows_in[u], 16)

            def add_rows(e, u):
                need(pool, added, 16 * SJ * e)
                pool.tensor_copy(si[:, :], add_at[:, bass.ds(e * SJ, SJ)]).then_inc(si_ready, 1)
                index_copied = pool.to_reg(e + 1)
                apart(pool)
                pool.wait_ge(si_ready, index_copied)
                for j in range(SJ):
                    rows_written = pool.to_reg(SJ * e + j + 1)
                    apart(pool)
                    pool.wait_ge(y_ready, rows_written)
                    pool.indirect_dma_start(out=out, in_=yo[u][:, j, :], in_offset=None,
                                            out_offset=bass.IndirectOffsetOnAxis(ap=si[:, j:j + 1], axis=0),
                                            bounds_check=NTOK + CAP - 1, oob_is_err=True,
                                            compute_op=ALU.add).then_inc(added, 16)

            pool.wait_ge(table_out, 32)
            pool.wait_ge(pads_out, 16)
            gather(0, 0)
            gather(1, 1)
            pool.wait_ge(base_out, 16)
            add_rows(0, 0)
            gather(2, 0)
            add_rows(1, 1)
            gather(3, 1)
            with pool.Fori(2, E // 2) as it:
                add_rows(2 * it - 2, 0)
                gather(2 * it, 0)
                add_rows(2 * it - 1, 1)
                gather(2 * it + 1, 1)
            add_rows(E - 2, 0)
            add_rows(E - 1, 1)
            pool.wait_ge(added, 16 * SJ * E)

        @block.scalar
        def _(act):
            act.wait_ge(c_in, 16)
            act.wait_ge(w_in, 16 * W_LOADS)
            for hh in range(HEADS):
                act.activation(decay[:, hh, :], col("diff", BLK), ACT.Exp,
                               scale=ls_s[:, hh:hh + 1]).then_inc(exp_ready, 1)

            with act.Fori(0, ROUNDS) as it:
                for u in range(RING):
                    t = RING * it + u
                    act.wait_ge(xn_turned, t + 1)
                    act.activation(xnT[:, :, bass.ds(t * P, P)],
                                   ps_t[u][0:HALF, 0:2 * P].rearrange("p (f n) -> p f n", f=2),
                                   ACT.Copy).then_inc(xnT_ready, 1)

            act.wait_ge(vp_zero, 2)

            def q_out(c, w, f):
                act.wait_ge(proj_done, 6 * c + f + 1)
                need(act, energy_done, CB * (c - 1))
                for odd in range(2):
                    ins = act.activation(qm[w][f][:, odd, :], ps_proj[f][0:HALF, 0:CHUNK], ACT.Silu,
                                         scale=cst[0:HALF, _C["mask"].start + odd:_C["mask"].start + odd + 1])
                ins.then_inc(proj_taken, 1)

            def k_out(c, w, f):
                act.wait_ge(proj_done, 6 * c + f + 3)
                if f:
                    act.activation(g1[w][HALF:HALF + G, :], ps_proj[f][HALF:HALF + G, 0:CHUNK],
                                   ACT.Copy).then_inc(g1_ready, 1)
                act.activation(kT[w][f][:, :], ps_proj[f][0:HALF, 0:CHUNK], ACT.Silu).then_inc(proj_taken, 1)

            def v_out(n, w):
                act.wait_ge(v_done, n + 1)
                need(act, av_done, n - 1)
                act.activation(vp[w][:, :, :].rearrange("p j (x d) -> p j x d", d=HD)[:, :, 0:4:3, :],
                               ps_v[0:BLK, 0:D].rearrange("p (j x d) -> p j x d", x=2, d=HD),
                               ACT.Silu).then_inc(v_ready, 1)

            def gate_out(c, w, f):
                act.wait_ge(proj_done, 6 * c + f + 5)
                need(act, go_ready, 2 * (c - 1))
                act.activation(gate[w][:, f, :], ps_proj[f][0:HALF, 0:CHUNK], ACT.Tanh,
                               scale=0.5).then_inc(proj_taken, 1)

            def chunk_out(c, w):
                q_out(c, w, 0)
                q_out(c, w, 1)
                k_out(c, w, 0)
                k_out(c, w, 1)
                v_out(CB * c, 0)
                gate_out(c, w, 0)
                gate_out(c, w, 1)
                for i in range(1, CB):
                    v_out(CB * c + i, i % 2)

            chunk_out(0, 0)
            chunk_out(1, 1)
            with act.Fori(1, NCHUNK // 2) as it:
                chunk_out(2 * it, 0)
                chunk_out(2 * it + 1, 1)

            act.wait_ge(go_ready, 2 * NCHUNK)

            def take_tiles(it):
                for u in range(RING):
                    t = RING * it + u
                    need(act, wo_done, t - RING + 1)
                    act.activation(gos[u][:, :, :], goT[:, :, bass.ds(t * P, P)], ACT.Copy).then_inc(gos_ready, 1)

            def rows_out(it):
                for u in range(RING):
                    t = RING * it + u
                    act.wait_ge(xf_ready, t + 1)
                    act.activation(y1[u][:, :], xf[u][:, :], ACT.Square,
                                   accum_out=ssq[:, u:u + 1]).then_inc(ssq_ready, 1)
                for u in range(RING):
                    t = RING * it + u
                    act.wait_ge(xf_turned, t + 1)
                    act.activation(xfT[u][:, :, :], ps_t[u][0:HALF, 0:2 * P].rearrange("p (f n) -> p f n", f=2),
                                   ACT.Copy).then_inc(xfT_ready, 1)
                act.wait_ge(rms_ready, it + 1)
                for u in range(RING):
                    t = RING * it + u
                    act.activation(zrow[:, bass.ds(t, 1), E:ROW].squeeze(1), xf[u][:, :], ACT.Copy,
                                   scale=rms[:, bass.ds(t, 1)]).then_inc(zn_ready, 1)

            take_tiles(0)
            with act.Fori(1, ROUNDS) as it:
                take_tiles(it)
                rows_out(it - 1)
            rows_out(ROUNDS - 1)

            act.wait_ge(ex_ready, 1)
            act.activation(probs[:, :, :], ex[:, :, :], ACT.Exp).then_inc(probs_exp, 1)

            def split_hi(e, u):
                act.wait_ge(we_in[u], 16 * 3 * (half_of(e, u) + 1))
                need(act, u_done, 8 * e)
                act.activation(wA_hi[:, :], wA[:, :], ACT.Copy, scale=nwA[:, bass.ds(e, 1)]).then_inc(w_hi, 1)
                act.activation(wB_hi[:, :], wB[:, :], ACT.Copy, scale=nwB[:, bass.ds(e, 1)]).then_inc(w_hi, 1)
                for i in range(4):
                    act.wait_ge(z_turned, 4 * e + i + 1)
                    cols = slice(i // 2 * MOV, (i // 2 + 1) * MOV)
                    act.activation((zB if i % 2 else zA_hi)[:, cols], ps_z[i % 2][:, 0:MOV],
                                   ACT.Copy).then_inc(z_hi, 1)

            def silus(e):
                for s in range(2 * HC):
                    act.wait_ge(g_done, 8 * e + s + 1)
                    need(act, a_ready, 8 * e + s - 1)
                    act.activation(silu_g[s % 2], ps_g[s % 2][:, 0:MOV], ACT.Silu).then_inc(silu_ready, 1)

            def weigh(e, u):
                act.wait_ge(wslot_ready, e + 1)
                need(act, added, 16 * SJ * (e - 1))
                for j in range(SJ):
                    act.wait_ge(ffn_done, SJ * e + j + 1)
                    act.activation(yo[u][:, j, :], ps_y[j % 2][0:SP_, 0:D], ACT.Copy,
                                   scale=wslot[u][:, j:j + 1]).then_inc(y_ready, 1)

            def between(e, u):
                split_hi(e + 1, 1 - u)
                weigh(e, u)
                silus(e + 1)

            split_hi(0, 0)
            silus(0)
            between(0, 0)
            with act.Fori(0, E // 2 - 1) as it:
                between(2 * it + 1, 1)
                between(2 * it + 2, 0)
            weigh(E - 1, 1)

        @block.vector
        def _(dve):
            dve.wait_ge(w_in, 16 * W_LOADS)

            def norm_round(it):
                for u in range(RING):
                    t = RING * it + u
                    dve.wait_ge(embed_done, t + 1)
                    dve.tensor_tensor(h[:, bass.ds(t, 1), :].squeeze(1), ps_h[u][:, 0:D], b_s[:, :],
                                      ALU.add).then_inc(h_ready, 1)
                    apart(dve)
                    dve.wait_ge(h_ready, t + 1)
                    dve.bn_stats(st[u][:, :], h[:, bass.ds(t, 1), :].squeeze(1)).then_inc(st_ready, 1)
                    apart(dve)
                    dve.wait_ge(st_ready, t + 1)
                    dve.bn_aggr(mv[:, u, :], st[u][:, :]).then_inc(mv_ready, 1)
                dve.wait_ge(mv_ready, RING * (it + 1))
                dve.tensor_scalar(ve[:, :], mv[:, :, 1], EPS_LN, None, ALU.add).then_inc(ve_ready, 1)
                dve.wait_ge(rstd_ready, it + 1)
                for u in range(RING):
                    t = RING * it + u
                    need(dve, xn_turned, t - RING + 1)
                    dve.tensor_scalar(xn[u][:, :], h[:, bass.ds(t, 1), :].squeeze(1), mv[:, u, 0:1],
                                      rstd[:, u:u + 1], ALU.subtract, ALU.mult).then_inc(xn_ready, 1)

            norm_round(0)
            with dve.Fori(1, ROUNDS) as it:
                norm_round(it)

            dve.wait_ge(exp_ready, HEADS)
            dve.tensor_tensor(decay[:, :, :], decay[:, :, :],
                              col("keep", BLK).unsqueeze(1).broadcast_to([BLK, HEADS, BLK]),
                              ALU.mult).then_inc(decay_ready, 1)
            dve.tensor_scalar(wo_h[:, :, :], wo_s[:, :, :], 0.5, None, ALU.mult).then_inc(woh_ready, 1)
            dve.wait_ge(decay_ready, 1)
            decay_v = decay[:, :, :].rearrange("p (f j x) n -> p f j (x n)", f=2, j=PAIRS)

            def chunk_mul(c, w):
                for i in range(CB):
                    n = CB * c + i
                    dve.wait_ge(energy_done, n + 1)
                    need(dve, av_done, n - 1)
                    dve.tensor_tensor(ed[i % 2][:, :, :, :],
                                      trio[0:BLK, :, 0:4 * BLK].rearrange("p j (f n) -> p f j n", f=2),
                                      decay_v, ALU.mult).then_inc(ed_ready, 1)
                dve.wait_ge(av_done, CB * (c + 1))
                dve.wait_ge(proj_taken, 6 * (c + 1))
                for f in range(2):
                    dve.scalar_tensor_tensor(goT[:, f, bass.ds(c * CHUNK, CHUNK)], gate[w][:, f, :], 1.0,
                                             ps_o[f][0:HALF, 0:CHUNK], ALU.add, ALU.mult).then_inc(go_ready, 1)

            chunk_mul(0, 0)
            chunk_mul(1, 1)
            with dve.Fori(1, NCHUNK // 2) as it:
                chunk_mul(2 * it, 0)
                chunk_mul(2 * it + 1, 1)

            dve.wait_ge(hb_ready, NT)

            def attn_norm(it):
                for u in range(RING):
                    t = RING * it + u
                    apart(dve)
                    dve.wait_ge(wo_done, t + 1)
                    dve.bn_stats(st[u][:, :], ps_w[u][:, 0:D]).then_inc(stw_ready, 1)
                    apart(dve)
                    dve.wait_ge(stw_ready, t + 1)
                    dve.bn_aggr(mv[:, u, :], st[u][:, :]).then_inc(mvw_ready, 1)
                dve.wait_ge(mvw_ready, RING * (it + 1))
                dve.tensor_scalar(ve[:, :], mv[:, :, 1], EPS_LN, None, ALU.add).then_inc(vew_ready, 1)
                dve.wait_ge(rstdw_ready, it + 1)
                need(dve, ssq_ready, RING * it)
                for u in range(RING):
                    dve.tensor_scalar(y1[u][:, :], ps_w[u][:, 0:D], mv[:, u, 0:1], rstd[:, u:u + 1],
                                      ALU.subtract, ALU.mult).then_inc(y1_ready, 1)

            def out_norm(it):
                for u in range(RING):
                    t = RING * it + u
                    apart(dve)
                    dve.wait_ge(h2_ready, t + 1)
                    dve.bn_stats(st2[u][:, :], h[:, bass.ds(t, 1), :].squeeze(1)).then_inc(st2_ready, 1)
                    apart(dve)
                    dve.wait_ge(st2_ready, t + 1)
                    dve.bn_aggr(mv2[:, u, :], st2[u][:, :]).then_inc(mv2_ready, 1)
                dve.wait_ge(mv2_ready, RING * (it + 1))
                dve.tensor_scalar(ve2[:, :], mv2[:, :, 1], EPS_LN, None, ALU.add).then_inc(ve2_ready, 1)
                dve.wait_ge(rstd2_ready, it + 1)
                for u in range(RING):
                    t = RING * it + u
                    need(dve, zn_ready, t - RING + 1)
                    need(dve, xf_turned, t - RING + 1)
                    dve.tensor_scalar(xf[u][:, :], h[:, bass.ds(t, 1), :].squeeze(1),
                                      mv2[:, u, 0:1], rstd2[:, u:u + 1], ALU.subtract,
                                      ALU.mult).then_inc(xf_ready, 1)
                dve.wait_ge(ssq_ready, RING * (it + 1))
                dve.tensor_scalar(ve3[:, :], ssq[:, :], 1.0 / D, EPS_FFN / 4, ALU.mult,
                                  ALU.add).then_inc(ve3_ready, 1)

            attn_norm(0)
            out_norm(0)
            with dve.Fori(1, ROUNDS) as it:
                attn_norm(it)
                out_norm(it)

            steps = [0]

            def link(ins):
                steps[0] += 1
                ins.then_inc(route_step, 1)
                dve.wait_ge(route_step, steps[0])

            def per_expert(a):
                return a.unsqueeze(1).broadcast_to([P, E, NT])

            def by_tile(a):
                return a.rearrange("p e t -> p t e")

            def per_tile(name):
                return col(name).unsqueeze(2).broadcast_to([P, E, NT])

            lg = ps_l[:, 0:E * NT].rearrange("p (e t) -> p e t", e=E)
            dve.wait_ge(logits_done, NT)
            link(dve.tensor_reduce(top[:, :], by_tile(lg), AX_X, ALU.max))
            dve.tensor_tensor(ex[:, :, :], lg, per_expert(top[:, :]), ALU.subtract).then_inc(ex_ready, 1)
            dve.wait_ge(probs_exp, 1)
            link(dve.tensor_reduce(rank[:, :], by_tile(probs[:, :, :]), AX_X, ALU.add))
            link(dve.reciprocal(top[:, :], rank[:, :]))
            link(dve.tensor_tensor(left[:, :, :], probs[:, :, :], per_expert(top[:, :]), ALU.mult))
            for k in range(2):
                link(dve.tensor_reduce(best[:, k, :], by_tile(left[:, :, :]), AX_X, ALU.max))
                link(dve.tensor_tensor(same[:, :, :], left[:, :, :], per_expert(best[:, k, :]), ALU.is_equal))
                link(dve.tensor_tensor(cnt[:, :, :], same[:, :, :], per_tile("rank"), ALU.mult))
                link(dve.tensor_reduce(rank[:, :], by_tile(cnt[:, :, :]), AX_X, ALU.max))
                link(dve.tensor_tensor(hot[:, k, :, :], cnt[:, :, :], per_expert(rank[:, :]), ALU.is_equal))
                if k == 0:
                    link(dve.scalar_tensor_tensor(left[:, :, :], hot[:, 0, :, :], -4.0, left[:, :, :], ALU.mult,
                                                  ALU.add))
            link(dve.tensor_tensor(cnt[:, :, :], hot[:, 0, :, :], hot[:, 1, :, :], ALU.add))
            link(dve.tensor_tensor_scan(upto[:, :, :].rearrange("p e t -> p (e t)"), col("reset"),
                                        cnt[:, :, :].rearrange("p e t -> p (e t)"), 0.0, ALU.mult, ALU.add))
            dve.tensor_tensor(upto[:, :, :], upto[:, :, :], cnt[:, :, :], ALU.subtract).then_inc(counts_ready, 1)
            link(dve.tensor_tensor(top[:, :], best[:, 0, :], best[:, 1, :], ALU.add))
            link(dve.reciprocal(cws[:, :], top[:, :]))
            link(dve.tensor_tensor(cw[:, :, :], best[:, :, :], cws[:, :].unsqueeze(1).broadcast_to([P, 2, NT]),
                                   ALU.mult))
            for k in range(2):
                link(dve.tensor_tensor(pick[:, k, :, :], hot[:, k, :, :], per_tile("expert"), ALU.mult))
                link(dve.tensor_reduce(exp_of[:, k, :], by_tile(pick[:, k, :, :]), AX_X, ALU.add))
            dve.wait_ge(places_done, 1)
            for k in range(2):
                link(dve.tensor_tensor(pick[:, k, :, :], hot[:, k, :, :],
                                       ps_d[:, 0:E * NT].rearrange("p (e t) -> p e t", e=E), ALU.mult))
                link(dve.tensor_reduce(pos[:, k, :], by_tile(pick[:, k, :, :]), AX_X, ALU.add))
            link(dve.tensor_scalar(kept[:, :, :], pos[:, :, :], float(CAP), None, ALU.is_lt))
            link(dve.tensor_scalar(jj[:, :, :], pos[:, :, :], float(SP_), None, ALU.is_ge))
            for i in range(2, SJ):
                link(dve.scalar_tensor_tensor(jj[:, :, :], pos[:, :, :], float(i * SP_), jj[:, :, :], ALU.is_ge,
                                              ALU.add))
            link(dve.scalar_tensor_tensor(pl[:, :, :], jj[:, :, :], -float(SP_), pos[:, :, :], ALU.mult, ALU.add))
            link(dve.scalar_tensor_tensor(ej[:, :, :], exp_of[:, :, :], float(SJ), jj[:, :, :], ALU.mult, ALU.add))
            link(dve.tensor_scalar(far[:, :, :], kept[:, :, :], -FAR, FAR, ALU.mult, ALU.add))
            link(dve.tensor_tensor(ej[:, :, :], ej[:, :, :], far[:, :, :], ALU.add))
            for k in range(2):
                mine = slice(k * NT, (k + 1) * NT)
                link(dve.tensor_tensor(hot_e[:, mine, 1, :],
                                       col("slot_ej").unsqueeze(1).broadcast_to([P, NT, E * SJ]),
                                       ej[:, k, :].unsqueeze(2).broadcast_to([P, NT, E * SJ]), ALU.is_equal))
                link(dve.tensor_scalar(hot_e[:, mine, 0, :], hot_e[:, mine, 1, :], col("part"), None, ALU.mult))
                link(dve.tensor_tensor(hot_e[:, mine, 1, :], hot_e[:, mine, 1, :],
                                       col("tile1").unsqueeze(2).broadcast_to([P, NT, E * SJ]), ALU.mult))
                dve.tensor_tensor(hot_p[:, mine, :], col("slot_p").unsqueeze(1).broadcast_to([P, NT, SP_]),
                                  pl[:, k, :].unsqueeze(2).broadcast_to([P, NT, SP_]),
                                  ALU.is_equal).then_inc(hots_ready, 1)
            link(dve.tensor_tensor(cw[:, :, :], cw[:, :, :], kept[:, :, :], ALU.mult))
            for k in range(2):
                link(dve.tensor_tensor(pick[:, k, :, :], hot[:, k, :, :], per_expert(cw[:, k, :]), ALU.mult))
            dve.tensor_tensor(zrow[:, :, 0:E].rearrange("p t e -> p e t"), pick[:, 0, :, :], pick[:, 1, :, :],
                              ALU.add).then_inc(weights_ready, 1)
            dve.wait_ge(tokens_done, 1)
            link(dve.tensor_copy(tok_of[:, :], ps_s[0:SP_, 0:2 * E * SJ]))
            part_of, tile_of = tok_of[:, 0:E * SJ], tok_of[:, E * SJ:2 * E * SJ]
            link(dve.scalar_tensor_tensor(token[:, :], tile_of, float(P), part_of, ALU.mult, ALU.add))
            dve.tensor_scalar(gather_at[:, :], token[:, :], -float(P), 0.0, ALU.add, ALU.max).then_inc(index_ready, 1)
            link(dve.tensor_scalar(empty[:, :], tile_of, 0.0, None, ALU.is_equal))
            link(dve.tensor_tensor(empty[:, :], empty[:, :], col("slot_id", SP_), ALU.mult))
            dve.scalar_tensor_tensor(add_at[:, :], token[:, :], -float(P), empty[:, :], ALU.add,
                                     ALU.add).then_inc(index_ready, 1)
            link(dve.tensor_tensor(cws[:, :], cw[:, 0, :], cw[:, 1, :], ALU.add))
            link(dve.reciprocal(top[:, :], rms[:, :]))
            link(dve.tensor_tensor(cws[:, :], cws[:, :], top[:, :], ALU.mult))
            with dve.Fori(0, NT) as t:
                dve.scalar_tensor_tensor(h[:, bass.ds(t, 1), :].squeeze(1), zrow[:, bass.ds(t, 1), E:ROW].squeeze(1),
                                         cws[:, bass.ds(t, 1)], h[:, bass.ds(t, 1), :].squeeze(1), ALU.mult,
                                         ALU.add).then_inc(base_ready, 1)

            def split_lo(e, u):
                for i, (w, nw, hi, lo) in enumerate(((wA, nwA, wA_hi, wA_lo), (wB, nwB, wB_hi, wB_lo))):
                    n = P if i == 0 else TAIL
                    dve.wait_ge(w_hi, 2 * e + i + 1)
                    dve.scalar_tensor_tensor(lo[0:n, :], w[0:n, :], nw[0:n, bass.ds(e, 1)],
                                             hi[0:n, :].bitcast(F32), ALU.mult, ALU.subtract).then_inc(w_split, 1)
                for i in range(4):
                    cols = slice(i // 2 * MOV, (i // 2 + 1) * MOV)
                    dve.wait_ge(z_hi, 4 * e + i + 1)
                    if i % 2:
                        dve.tensor_tensor(zB[TAIL:P, cols], ps_z[1][TAIL:P, 0:MOV],
                                          zB[TAIL:P, cols].bitcast(F32), ALU.subtract).then_inc(z_split, 1)
                    else:
                        dve.tensor_tensor(zA_lo[:, cols], ps_z[0][:, 0:MOV], zA_hi[:, cols].bitcast(F32),
                                          ALU.subtract).then_inc(z_split, 1)
                need(dve, y_ready, SJ * (e - 1))
                dve.tensor_copy(wslot[u][:, :], zin[u][:, :, bass.ds(e, 1)].squeeze(2)).then_inc(wslot_ready, 1)

            def products(e):
                need(dve, ffn_done, SJ * e)
                for s in range(2 * HC):
                    sh, m = s // HC, s % HC
                    dve.wait_ge(silu_ready, 8 * e + s + 1)
                    dve.wait_ge(u_done, 8 * e + s + 1)
                    dve.tensor_tensor(act_h[:, m, sh * MOV:(sh + 1) * MOV], silu_g[s % 2], ps_u[s % 2][:, 0:MOV],
                                      ALU.mult).then_inc(a_ready, 1)

            split_lo(0, 0)
            products(0)
            split_lo(1, 1)
            products(1)
            with dve.Fori(1, E // 2) as it:
                split_lo(2 * it, 0)
                products(2 * it)
                split_lo(2 * it + 1, 1)
                products(2 * it + 1)

        @block.tensor
        def _(pe):
            ident = col("ident")
            pe.wait_ge(w_in, 16 * W_LOADS)
            pe.wait_ge(c_in, 16)

            def embed(it):
                for u in range(RING):
                    t = RING * it + u
                    pe.wait_ge(x_in[u], 16 * (it + 1))
                    need(pe, h_ready, t - RING + 1)
                    for k in range(KC):
                        mm = pe.matmul(ps_h[u][:, 0:D], xt[u][:, k, :], wT_s[:, k, :], start=(k == 0),
                                       stop=(k == KC - 1))
                    mm.then_inc(embed_done, 1)

            def turn_xn(it):
                for u in range(RING):
                    t = RING * it + u
                    pe.wait_ge(xn_ready, t + 1)
                    need(pe, xnT_ready, t - RING + 1)
                    for f in range(2):
                        mm = pe.transpose(ps_t[u][0:HALF, f * P:(f + 1) * P], xn[u][:, f * HALF:(f + 1) * HALF],
                                          ident)
                    mm.then_inc(xn_turned, 1)

            embed(0)
            embed(1)
            turn_xn(0)
            with pe.Fori(2, ROUNDS) as it:
                embed(it)
                turn_xn(it - 1)
            turn_xn(ROUNDS - 1)

            def project(c, w, i, M, weights):
                need(pe, proj_taken, 6 * c + i - 1)
                for f in range(2):
                    mm = pe.matmul(ps_proj[i % 2][0:M, 0:CHUNK], weights(f), xs[w][:, f, :], start=(f == 0),
                                   stop=(f == 1))
                mm.then_inc(proj_done, 1)

            def values(c, w, i):
                n = CB * c + i
                need(pe, v_ready, n)
                for f in range(2):
                    mm = pe.matmul(ps_v[0:BLK, 0:D], xs[w][:, f, i * BLK:(i + 1) * BLK], wv_s[:, f, :],
                                   start=(f == 0), stop=(f == 1))
                mm.then_inc(v_done, 1)

            def energy(c, w, i):
                n = CB * c + i
                need(pe, ed_ready, n)
                cols = slice(i * BLK, (i + 1) * BLK)
                for f in range(2):
                    for j in range(PAIRS):
                        rows = slice(32 * j, 32 * j + 32)
                        mm = pe.matmul(trio[0:BLK, j, f * 2 * BLK:(f + 1) * 2 * BLK], kT[w][f][rows, cols],
                                       qm[w][f][rows, :, cols], start=True, stop=True)
                mm.then_inc(energy_done, 1)

            def attend(c, w, i):
                n = CB * c + i
                pe.wait_ge(v_ready, n + 1)
                pe.wait_ge(ed_ready, n + 1)
                if i == 0:
                    need(pe, go_ready, 2 * c)
                for f in range(2):
                    for odd in range(2):
                        for j in range(PAIRS):
                            mm = pe.matmul(ps_o[f][32 * j:32 * j + 32, i * BLK:(i + 1) * BLK],
                                           vp[i % 2][:, PAIRS * f + j, 2 * HD * odd:2 * HD * (odd + 1)],
                                           ed[i % 2][:, f, j, odd * BLK:(odd + 1) * BLK], start=(odd == 0),
                                           stop=(odd == 1))
                mm.then_inc(av_done, 1)

            def chunk(c, w):
                pe.wait_ge(xs_ready, c + 1)
                for f in range(2):
                    project(c, w, f, HALF, lambda k: wq_s[:, k, f * HALF:(f + 1) * HALF])
                project(c, w, 2, HALF, lambda k: wkg_s[:, k, 0:HALF])
                project(c, w, 3, HALF + G, lambda k: wkg_s[:, k, HALF:D + G])
                values(c, w, 0)
                pe.wait_ge(g1_ready, c + 1)
                for f in range(2):
                    need(pe, proj_taken, 6 * c + f + 3)
                    pe.matmul(ps_proj[f][0:HALF, 0:CHUNK], wg2_s[HALF:HALF + G, f * HALF:(f + 1) * HALF],
                              g1[w][HALF:HALF + G, :], start=True, stop=True).then_inc(proj_done, 1)
                energy(c, w, 0)
                for i in range(1, CB):
                    values(c, w, i)
                    attend(c, w, i - 1)
                    energy(c, w, i)
                attend(c, w, CB - 1)

            chunk(0, 0)
            chunk(1, 1)
            with pe.Fori(1, NCHUNK // 2) as it:
                chunk(2 * it, 0)
                chunk(2 * it + 1, 1)

            pe.wait_ge(woh_ready, 1)

            def project_out(it):
                for u in range(RING):
                    t = RING * it + u
                    pe.wait_ge(gos_ready, t + 1)
                    need(pe, y1_ready, t - RING + 1)
                    for f in range(2):
                        mm = pe.matmul(ps_w[u][:, 0:D], gos[u][:, f, :], wo_h[:, f, :], start=(f == 0),
                                       stop=(f == 1))
                    mm.then_inc(wo_done, 1)

            lg_v = ps_l[:, 0:E * NT].rearrange("p (e t) -> p e t", e=E)

            def route(it):
                for u in range(RING):
                    t = RING * it + u
                    pe.wait_ge(xf_ready, t + 1)
                    need(pe, xfT_ready, t - RING + 1)
                    for f in range(2):
                        mm = pe.transpose(ps_t[u][0:HALF, f * P:(f + 1) * P],
                                          xf[u][:, f * HALF:(f + 1) * HALF], ident)
                    mm.then_inc(xf_turned, 1)
                for u in range(RING):
                    t = RING * it + u
                    pe.wait_ge(xfT_ready, t + 1)
                    for f in range(2):
                        mm = pe.matmul(lg_v[:, :, bass.ds(t, 1)].squeeze(2), xfT[u][:, f, :], gw_s[:, f, :],
                                       start=(f == 0), stop=(f == 1))
                    mm.then_inc(logits_done, 1)

            project_out(0)
            project_out(1)
            route(0)
            with pe.Fori(2, ROUNDS) as it:
                project_out(it)
                route(it - 1)
            route(ROUNDS - 1)

            pe.wait_ge(counts_ready, 1)
            pe.matmul(ps_d[:, 0:E * NT], col("tri"), cnt[:, :, :].rearrange("p e t -> p (e t)"), start=True,
                      stop=False)
            pe.matmul(ps_d[:, 0:E * NT], ones[:, :], upto[:, :, :].rearrange("p e t -> p (e t)"), start=False,
                      stop=True).then_inc(places_done, 1)
            for i in range(2 * NT):
                if i % NT == 0:
                    pe.wait_ge(hots_ready, i // NT + 1)
                mm = pe.matmul(ps_s[0:SP_, 0:2 * E * SJ], hot_p[:, i, :],
                               hot_e[:, i, :, :].rearrange("p x s -> p (x s)"), start=(i == 0),
                               stop=(i == 2 * NT - 1))
            mm.then_inc(tokens_done, 1)

            def turn_rows(e, u):
                pe.wait_ge(rows_in[u], 16 * SJ * (half_of(e, u) + 1))
                for i in range(4):
                    need(pe, z_split, 4 * e + i - 1)
                    for x in range(SJ // 2):
                        j = i // 2 * (SJ // 2) + x
                        if i % 2:
                            src = zin[u][:, j, E + P:TROW]
                        else:
                            src = zin[u][:, j, E:E + P]
                        mm = pe.transpose(ps_z[i % 2][:, x * SP_:(x + 1) * SP_], src, ident[0:SP_, 0:SP_])
                    mm.then_inc(z_turned, 1)

            def hidden(e):
                pe.wait_ge(w_split, 2 * (e + 1))
                pe.wait_ge(z_split, 4 * (e + 1))
                for s in range(2 * HC):
                    sh, m = s // HC, s % HC
                    need(pe, a_ready, 8 * e + s - 1)
                    cols = slice(sh * MOV, (sh + 1) * MOV)
                    for ps, at, done in ((ps_g, m * P, g_done), (ps_u, HID + m * P, u_done)):
                        rows = slice(at, at + P)
                        parts = ((wA_hi[:, rows], zA_hi[:, cols]), (wA_hi[:, rows], zA_lo[:, cols]),
                                 (wA_lo[:, rows], zA_hi[:, cols]), (wB_hi[:, rows], zB[:, cols]),
                                 (wB_lo[:, rows], zB[0:TAIL, cols]))
                        for i, (w, z) in enumerate(parts):
                            mm = pe.matmul(ps[s % 2][:, 0:MOV], w, z, start=(i == 0), stop=(i == len(parts) - 1))
                        mm.then_inc(done, 1)

            def ffn(e, u):
                pe.wait_ge(w2_in[u], 16 * (half_of(e, u) + 1))
                pe.wait_ge(a_ready, 8 * (e + 1))
                for j in range(SJ):
                    need(pe, y_ready, SJ * e + j - 1)
                    for c in range(HC):
                        mm = pe.matmul(ps_y[j % 2][0:SP_, 0:D], act_h[:, c, j * SP_:(j + 1) * SP_],
                                       w2_s[u][:, c, :], start=(c == 0), stop=(c == HC - 1))
                    mm.then_inc(ffn_done, 1)

            def between(e, u):
                turn_rows(e + 1, 1 - u)
                ffn(e, u)
                hidden(e + 1)

            turn_rows(0, 0)
            hidden(0)
            between(0, 0)
            with pe.Fori(0, E // 2 - 1) as it:
                between(2 * it + 1, 1)
                between(2 * it + 2, 0)
            ffn(E - 1, 1)


_INS = ["xT", "wT", "b", "ls", "wq", "wkg", "wv", "wg2", "wo", "lnw", "lnb", "gwT", "w13T", "w2T", "nwT", "const"]


def laid_out(x, W, b, ls, Wq, Wk, Wv, Wo, Wg1, Wg2, lnw, lnb, gate_w, w13, w2, norm_w):
    a = np.asarray
    patches = a(x).reshape(B_IMG, CH_IN, GRID, PATCH, GRID, PATCH).transpose(0, 2, 4, 3, 5, 1).reshape(NT, P, KC, P)
    return {
        "xT": np.ascontiguousarray(patches.transpose(0, 3, 2, 1)).reshape(NT * P, KC * P),
        "wT": np.ascontiguousarray(a(W).T), "b": a(b), "ls": a(ls), "wq": a(Wq),
        "wkg": np.concatenate([a(Wk), a(Wg1)], 1), "wv": a(Wv), "wg2": a(Wg2), "wo": a(Wo), "lnw": a(lnw),
        "lnb": a(lnb), "gwT": np.ascontiguousarray(a(gate_w).T),
        "w13T": np.ascontiguousarray(a(w13).transpose(0, 2, 1)).reshape(E * D, 2 * HID),
        "w2T": np.ascontiguousarray(a(w2).transpose(0, 2, 1)).reshape(E * HID, D),
        "nwT": np.ascontiguousarray(a(norm_w).T), "const": constants(),
    }


def kernel(**inputs):
    import concourse.bacc as _bacc
    from concourse.bass_utils import run_bass_kernel_spmd as _run

    i = inputs
    nc = _bacc.Bacc("TRN2", target_bir_lowering=False, num_devices=1)
    arrays = laid_out(i["x"], i["L0_tok_W"], i["L0_tok_b"], i["L0_attn_log_slope"], i["L0_attn_Wq"], i["L0_attn_Wk"],
                      i["L0_attn_Wv"], i["L0_attn_Wo"], i["L0_attn_Wg1"], i["L0_attn_Wg2"], i["L0_attn_ln_w"],
                      i["L0_attn_ln_b"], i["L0_ffn_gate_w"], i["L0_ffn_w13"], i["L0_ffn_w2"], i["L0_ffn_norm_w"])
    args = [nc.dram_tensor(n, arrays[n].shape, mybir.dt.from_np(arrays[n].dtype), kind="ExternalInput").ap()
            for n in _INS]
    args.append(nc.dram_tensor("out", (NTOK + CAP, D), F32, kind="ExternalOutput").ap())
    build(nc, *args)
    r = _run(nc, [arrays], core_ids=[0])
    return r.results[0]["out"][0:NTOK].reshape(B_IMG, SEQ, D)
```

```python
from contextlib import ExitStack

import numpy as np
import concourse.bass as bass
from concourse import mybir

F32 = mybir.dt.float32
F32R = mybir.dt.float32r
BF16 = mybir.dt.bfloat16
I32 = mybir.dt.int32
ALU = mybir.AluOpType
ACT = mybir.ActivationFunctionType
AX_X = mybir.AxisListType.X

P = 128
B_IMG, CH_IN, IMG, PATCH = 64, 3, 96, 16
GRID = IMG // PATCH
SEQ = GRID * GRID
NTOK = B_IMG * SEQ
FEAT = PATCH * PATCH * CH_IN
KC = FEAT // P
D = 192
HALF = D // 2
NT = NTOK // P
RING = 3
ROUNDS = NT // RING
HEADS = 12
HD = D // HEADS
G = 16
BLK = 2 * SEQ
CB = 4
CHUNK = CB * BLK
NCHUNK = NTOK // CHUNK
TC = 96
NTC = NTOK // TC
CT = CHUNK // TC
PAIRS = 3
E = 8
HID = 512
HC = HID // P
CAP = 720
SP_ = 120
SJ = CAP // SP_
MOV = CAP // 2
ROW = E + D
TAIL = D - P
TROW = ROW + TAIL
EPS_LN = 1e-5
EPS_FFN = 1e-6
FAR = 1000.0

_C = {}
_at = 0
for _name, _n in (("ident", P), ("tri", P), ("mask", 2), ("diff", BLK), ("keep", BLK), ("slot_p", SP_),
                  ("slot_ej", E * SJ), ("slot_id", E * SJ), ("expert", E), ("rank", E), ("reset", E * NTC),
                  ("tile1", NTC), ("part", 1)):
    _C[_name] = slice(_at, _at + _n)
    _at += _n
NCONST = _at


def constants():
    c = np.zeros((P, NCONST), np.float32)
    p = np.arange(P)
    c[:, _C["ident"]] = np.eye(P)
    c[:, _C["tri"]] = p[:, None] < p[None, :]
    c[:, _C["mask"]] = np.stack([p % 32 < 16, p % 32 >= 16], 1)
    m, n = np.arange(BLK)[:, None], np.arange(BLK)[None, :]
    keep = (n >= m) & (n // SEQ == m // SEQ)
    c[:BLK, _C["diff"]] = (n - m) * keep
    c[:BLK, _C["keep"]] = keep
    c[:, _C["slot_p"]] = np.arange(SP_)
    c[:, _C["slot_ej"]] = np.arange(E * SJ)
    c[:, _C["slot_id"]] = NTOK + TC + p[:, None] + SP_ * (np.arange(E * SJ) % SJ)[None, :]
    c[:, _C["expert"]] = np.arange(E)
    c[:, _C["rank"]] = E - np.arange(E)
    c[:, _C["reset"]] = (np.arange(E * NTC) % NTC) > 0
    c[:, _C["tile1"]] = np.arange(NTC) + 1
    c[:, _C["part"]] = p[:, None]
    return c


def build(nc, xT, wT, b, ls, wq, wkg, wv, wg2, wo, lnw, lnb, gwT, w13T, w2T, nwT, const, out):
    table = nc.dram_tensor("table", [NTOK, TROW], F32).ap()
    rows = nc.dram_tensor("rows", [NTOK, D], F32).ap()
    with ExitStack() as ctx:
        def sb(name, shape, dt=F32):
            return ctx.enter_context(nc.sbuf_tensor(name, shape, dt))

        def sem(name):
            return ctx.enter_context(nc.semaphore(name))

        def need(eng, s, value):
            if not (isinstance(value, int) and value <= 0):
                eng.wait_ge(s, value)

        cst = sb("cst", [P, NCONST])
        wT_s = sb("wT_s", [P, KC, D])
        b_s = sb("b_s", [P, D])
        ls_s = sb("ls_s", [BLK, HEADS])
        wq_s = sb("wq_s", [HALF, 2, D])
        wkg_s = sb("wkg_s", [HALF, 2, D + G])
        wv_s = sb("wv_s", [HALF, 2, D])
        wg2_s = sb("wg2_s", [HALF + G, D])
        wo_s = sb("wo_s", [HALF, 2, D])
        wo_h = sb("wo_h", [HALF, 2, D])
        lnw_s = sb("lnw_s", [P, D])
        lnb_s = sb("lnb_s", [P, D])
        gw_s = sb("gw_s", [HALF, 2, E])
        nwA = sb("nwA", [P, E])
        nwB = sb("nwB", [P, E])
        ones = sb("ones", [P, P])
        mhalf = sb("mhalf", [P, RING])

        hold0 = sb("hold0", [P, RING * KC * P])
        hold1 = sb("hold1", [P, 2 * NTOK])
        hold2 = sb("hold2", [P, 2 * NTC * SP_ // 2 + 2 * NTC * E * SJ])
        hold3 = sb("hold3", [P, 17 * CHUNK + 2 * TC * 2 * PAIRS])

        xt = [hold0[:, u * KC * P:(u + 1) * KC * P].rearrange("p (k n) -> p k n", k=KC) for u in range(RING)]
        h = hold2[:, 0:NT * D].rearrange("p (t d) -> p t d", d=D)
        xn = [sb(f"xn{u}", [P, D]) for u in range(RING)]
        st = [sb(f"st{u}", [P, 6]) for u in range(RING)]
        mv = sb("mv", [P, RING, 2])
        ve = sb("ve", [P, RING])
        rstd = sb("rstd", [P, RING])
        xnT = hold1[0:HALF, :].rearrange("p (f n) -> p f n", f=2)

        def chunk_place(parts, i, n=1):
            return hold3[0:parts, i * CHUNK:(i + n) * CHUNK]

        xs = [chunk_place(HALF, 2 * w, 2).rearrange("p (f n) -> p f n", f=2) for w in range(2)]
        qm = [[chunk_place(HALF, 4 + 4 * w + 2 * f, 2).rearrange("p (x n) -> p x n", x=2) for f in range(2)]
              for w in range(2)]
        g1 = [chunk_place(HALF + G, 12 + w) for w in range(2)]
        ed = chunk_place(BLK, 14, 3).rearrange("p (f j n) -> p f j n", f=2, j=PAIRS)
        kT = [[sb(f"kT{w}{f}", [HALF, CHUNK]) for f in range(2)] for w in range(2)]
        gate = [sb(f"gate{w}", [HALF, 2, CHUNK]) for w in range(2)]
        gos = [sb(f"gos{w}", [HALF, 2, CHUNK]) for w in range(2)]
        decay = sb("decay", [BLK, HEADS, BLK])
        vp = [sb(f"vp{w}", [BLK, 2 * PAIRS, 4 * HD]) for w in range(2)]

        h2 = sb("h2", [TC, NTC, D])
        y1 = sb("y1", [TC, CT, D])
        y2 = sb("y2", [TC, CT, D])
        squares = sb("squares", [TC, CT, D])
        stw = sb("stw", [TC, CT, 6])
        mvw = sb("mvw", [TC, CT, 2])
        vew = sb("vew", [TC, CT])
        rstdw = sb("rstdw", [TC, CT])
        sth = sb("sth", [TC, CT, 6])
        mv2 = sb("mv2", [TC, CT, 2])
        ve2 = sb("ve2", [TC, CT])
        rstd2 = sb("rstd2", [TC, CT])
        ssq = sb("ssq", [TC, CT])
        ve3 = sb("ve3", [TC, CT])
        rms = sb("rms", [TC, NTC])
        xf = sb("xf", [TC, CT, D])
        xfT = sb("xfT", [HALF, 2, CT, TC])
        lgT = hold2[0:E, NTC * SP_:NTC * SP_ + NTOK]
        zrow = sb("zrow", [TC, NTC, ROW])

        top = sb("top", [TC, NTC])
        ex = sb("ex", [TC, E, NTC])
        probs = sb("probs", [TC, E, NTC])
        left = sb("left", [TC, E, NTC])
        same = sb("same", [TC, E, NTC])
        best = sb("best", [TC, 2, NTC])
        rank = sb("rank", [TC, NTC])
        hot = sb("hot", [TC, 2, E, NTC])
        cnt = sb("cnt", [TC, E, NTC])
        upto = sb("upto", [TC, E, NTC])
        pick = sb("pick", [TC, 2, E, NTC])
        pos = sb("pos", [TC, 2, NTC])
        exp_of = sb("exp_of", [TC, 2, NTC])
        kept = sb("kept", [TC, 2, NTC])
        cw = sb("cw", [TC, 2, NTC])
        cws = sb("cws", [TC, NTC])
        jj = sb("jj", [TC, 2, NTC])
        pl = sb("pl", [TC, 2, NTC])
        ej = sb("ej", [TC, 2, NTC])
        far = sb("far", [TC, 2, NTC])
        hot_p = hold2[0:TC, 0:2 * NTC * SP_ // 2].bitcast(BF16).rearrange("p (c s) -> p c s", s=SP_)
        at = 2 * NTC * SP_ // 2
        hot_e = hold2[0:TC, at:at + 2 * NTC * E * SJ].bitcast(BF16).rearrange("p (c x s) -> p c x s", x=2, s=E * SJ)
        tok_of = sb("tok_of", [SP_, 2 * E * SJ])
        token = sb("token", [SP_, E * SJ])
        empty = sb("empty", [SP_, E * SJ])
        gather_at = sb("gather_at", [SP_, E * SJ], I32)
        add_at = sb("add_at", [SP_, E * SJ], I32)

        act_h = hold1[:, 0:HC * CAP].rearrange("p (c n) -> p c n", c=HC)
        silu_g = [hold1[:, HC * CAP + s * MOV:HC * CAP + (s + 1) * MOV] for s in range(2)]
        wA, wB = (hold3[:, i * 2 * HID:(i + 1) * 2 * HID] for i in range(2))
        wA_hi = sb("wA_hi", [P, 2 * HID], F32R)
        wA_lo = sb("wA_lo", [P, 2 * HID], F32R)
        wB_hi = sb("wB_hi", [P, 2 * HID], F32R)
        wB_lo = sb("wB_lo", [TAIL, 2 * HID], F32R)
        w2_s = [hold3[:, 4 * HID + u * HC * D:4 * HID + (u + 1) * HC * D].rearrange("p (c d) -> p c d", c=HC)
                for u in range(2)]
        at = 4 * HID + 2 * HC * D
        zin = [sb("zin0", [SP_, SJ, TROW]),
               hold3[0:SP_, at:at + SJ * TROW].rearrange("p (j d) -> p j d", j=SJ)]
        zA_hi = sb("zA_hi", [P, CAP], F32R)
        zA_lo = sb("zA_lo", [P, CAP], F32R)
        zB = sb("zB", [P, CAP], F32R)
        wslot = [sb(f"wslot{u}", [SP_, SJ]) for u in range(2)]
        yo = [hold0[0:SP_, u * SJ * D:(u + 1) * SJ * D].rearrange("p (j d) -> p j d", j=SJ) for u in range(2)]
        gi = [sb(f"gi{u}", [SP_, SJ], I32) for u in range(2)]
        si = sb("si", [SP_, SJ], I32)

        bank = [ctx.enter_context(nc.psum_tensor(f"bank{i}", [P, 512], F32)) for i in range(5)]
        trio = ctx.enter_context(nc.psum_tensor("trio", [P, 3, 512], F32))
        ps_h = [bank[2], bank[3], bank[4]]
        ps_t = [trio[:, u, :] for u in range(RING)]
        ps_ring = [bank[0], bank[1]]
        ps_w = [bank[2][0:TC, 0:D], bank[2][0:TC, D:2 * D], bank[3][0:TC, 0:D]]
        ps_o = bank[4]
        ps_l = bank[4]
        ps_d = bank[4]
        ps_s = bank[0]
        ps_z = [bank[0], bank[1]]
        ps_g = [bank[2], bank[3]]
        ps_u = [bank[4], trio[:, 0, :]]
        ps_y = [trio[:, 1, :], trio[:, 2, :]]

        c_in = sem("c_in")
        wT_in = sem("wT_in")
        w_in = sem("w_in")
        x_in = [sem(f"x_in{u}") for u in range(RING)]
        pads_out = sem("pads_out")
        ones_set = sem("ones_set")
        embed_done = sem("embed_done")
        h_ready = sem("h_ready")
        st_ready = sem("st_ready")
        mv_ready = sem("mv_ready")
        ve_ready = sem("ve_ready")
        rstd_ready = sem("rstd_ready")
        xn_ready = sem("xn_ready")
        xn_turned = sem("xn_turned")
        xnT_ready = sem("xnT_ready")
        exp_ready = sem("exp_ready")
        decay_ready = sem("decay_ready")
        woh_ready = sem("woh_ready")
        vp_zero = sem("vp_zero")
        rows_out = sem("rows_out")
        rows_back = sem("rows_back")
        xs_ready = sem("xs_ready")
        ring_full = sem("ring_full")
        ring_taken = sem("ring_taken")
        g1_ready = sem("g1_ready")
        energy_done = sem("energy_done")
        ed_ready = sem("ed_ready")
        av_done = sem("av_done")
        go_ready = sem("go_ready")
        hb_ready = sem("hb_ready")
        wo_done = sem("wo_done")
        stw_ready = sem("stw_ready")
        mvw_ready = sem("mvw_ready")
        vew_ready = sem("vew_ready")
        rstdw_ready = sem("rstdw_ready")
        y1_ready = sem("y1_ready")
        y2_ready = sem("y2_ready")
        h2_ready = sem("h2_ready")
        st2_ready = sem("st2_ready")
        mv2_ready = sem("mv2_ready")
        ve2_ready = sem("ve2_ready")
        rstd2_ready = sem("rstd2_ready")
        xf_ready = sem("xf_ready")
        ssq_ready = sem("ssq_ready")
        ve3_ready = sem("ve3_ready")
        rms_ready = sem("rms_ready")
        zn_ready = sem("zn_ready")
        lg_turned = sem("lg_turned")
        ex_ready = sem("ex_ready")
        probs_exp = sem("probs_exp")
        route_step = sem("route_step")
        counts_ready = sem("counts_ready")
        places_done = sem("places_done")
        hots_ready = sem("hots_ready")
        tokens_done = sem("tokens_done")
        index_ready = sem("index_ready")
        weights_ready = sem("weights_ready")
        base_ready = sem("base_ready")
        table_out = sem("table_out")
        base_out = sem("base_out")
        we_in = [sem(f"we_in{u}") for u in range(2)]
        w2_in = [sem(f"w2_in{u}") for u in range(2)]
        rows_in = [[sem(f"rows_in{u}{half}") for half in range(2)] for u in range(2)]
        gi_ready = sem("gi_ready")
        si_ready = sem("si_ready")
        w_hi = sem("w_hi")
        w_split = sem("w_split")
        z_turned = sem("z_turned")
        z_hi = sem("z_hi")
        z_split = sem("z_split")
        wslot_ready = sem("wslot_ready")
        g_done = sem("g_done")
        u_done = sem("u_done")
        silu_ready = sem("silu_ready")
        a_ready = sem("a_ready")
        ffn_done = sem("ffn_done")
        y_ready = sem("y_ready")
        added = sem("added")

        def apart(eng):
            eng.wait_ge(c_in, 16)

        def in_register(eng, value):
            return value if isinstance(value, int) else eng.to_reg(value)

        def half_of(e, u):
            return (e - u) // 2

        def col(name, rows=P):
            return cst[0:rows, _C[name]]

        def colt(name):
            return col(name, TC)

        W_LOADS = 13

        FULL = ("v1", "q0", "v2", "q1", "k1", "v3", "k0", "g0", "t0", "v0", "t2", "g1", "lg")
        ITEMS = {0: ("q0", "q1", "k1", "k0", "g0", "v0", "g1"),
                 1: tuple(n for n in FULL if n not in ("t0", "t2", "lg")),
                 NCHUNK: ("v1", "v2", "v3", "t0", "t2", "lg"), NCHUNK + 1: ("t0", "t2", "lg")}
        BEFORE = len(ITEMS[0]) + len(ITEMS[1])

        def ring(s, w, name):
            if isinstance(s, int) and s < 2:
                n = ITEMS[s].index(name) + (len(ITEMS[0]) if s else 0)
                return n, n % 2
            if isinstance(s, int) and s >= NCHUNK:
                n = BEFORE + len(FULL) * (NCHUNK - 2) + ITEMS[s].index(name)
                n += len(ITEMS[NCHUNK]) if s > NCHUNK else 0
                return n, n % 2
            i = FULL.index(name)
            return len(FULL) * (s - 2) + BEFORE + i, (len(FULL) * w + BEFORE + i) % 2

        def items_before(s, w):
            return ring(s, w, ITEMS[s][0] if isinstance(s, int) and s in ITEMS else FULL[0])[0]

        SINCE_K, SINCE_V = 3, 1

        def steps_of(eng, step):
            step(0, 0)
            step(1, 1)
            with eng.Fori(1, NCHUNK // 2) as it:
                step(2 * it, 0)
                step(2 * it + 1, 1)
            step(NCHUNK, 0)
            step(NCHUNK + 1, 1)

        def parts_of(s):
            if not isinstance(s, int):
                return True, True, True
            return s < NCHUNK, 1 <= s <= NCHUNK, s >= 2

        block = ctx.enter_context(nc.Block())

        @block.sync
        def _(sp):
            def load_x(it):
                for u in range(RING):
                    t = RING * it + u
                    need(sp, embed_done, t - RING + 1)
                    sp.dma_start(hold0[:, u * KC * P:(u + 1) * KC * P],
                                 xT[bass.ds(t * P, P), :]).then_inc(x_in[u], 16)

            sp.dma_start(wT_s[:, :, :], wT.rearrange("(k p) d -> p k d", p=P)).then_inc(wT_in, 16)
            load_x(0)
            sp.dma_start(cst[:, :], const).then_inc(c_in, 16)
            sp.dma_start(b_s[:, :], b.partition_broadcast(P)).then_inc(w_in, 16)
            sp.dma_start(ls_s[:, :], ls.partition_broadcast(BLK)).then_inc(w_in, 16)
            sp.dma_start(wq_s[:, :, :], wq.rearrange("(f p) d -> p f d", p=HALF)).then_inc(w_in, 16)
            sp.dma_start(wkg_s[:, :, :], wkg.rearrange("(f p) d -> p f d", p=HALF)).then_inc(w_in, 16)
            sp.dma_start(wv_s[:, :, :], wv.rearrange("(f p) d -> p f d", p=HALF)).then_inc(w_in, 16)
            sp.dma_start(wg2_s[HALF:HALF + G, :], wg2).then_inc(w_in, 16)
            sp.dma_start(wo_s[:, :, :], wo.rearrange("(f p) d -> p f d", p=HALF)).then_inc(w_in, 16)
            sp.dma_start(lnw_s[:, :], lnw.partition_broadcast(P)).then_inc(w_in, 16)
            sp.dma_start(lnb_s[:, :], lnb.partition_broadcast(P)).then_inc(w_in, 16)
            sp.dma_start(gw_s[:, :, :], gwT.rearrange("(f p) e -> p f e", p=HALF)).then_inc(w_in, 16)
            sp.dma_start(nwA[:, :], nwT[0:P, :]).then_inc(w_in, 16)
            for f in range(2):
                sp.dma_start(nwB[f * TAIL:(f + 1) * TAIL, :], nwT[P:D, :]).then_inc(w_in, 16)
            rows_v = rows.rearrange("(t p) d -> p t d", p=P)
            with sp.Fori(1, ROUNDS) as it:
                load_x(it)
                sp.wait_ge(h_ready, RING * it)
                sp.dma_start(rows_v[:, bass.ds(RING * it - RING, RING), :],
                             h[:, bass.ds(RING * it - RING, RING), :]).then_inc(rows_out, 16)
            sp.wait_ge(h_ready, NT)
            sp.dma_start(rows_v[:, NT - RING:NT, :], h[:, NT - RING:NT, :]).then_inc(rows_out, 16)
            sp.wait_ge(rows_out, 16 * ROUNDS)
            sp.dma_start(h2[:, :, :], rows.rearrange("(t p) d -> p t d", p=TC)).then_inc(rows_back, 16)
            sp.wait_ge(ones_set, 3)
            sp.dma_start(out[NTOK:NTOK + CAP, :].rearrange("(p j) d -> p j d", j=SJ),
                         zin[0][:, :, 0:D]).then_inc(pads_out, 16)

            def load_expert(e, u):
                need(sp, w_split, 2 * e)
                sp.dma_start(wA[:, :], w13T[bass.ds(e * D, P), :]).then_inc(we_in[u], 16)
                for f in range(2):
                    sp.dma_start(wB[f * TAIL:(f + 1) * TAIL, :],
                                 w13T[bass.ds(e * D + P, TAIL), :]).then_inc(we_in[u], 16)
                need(sp, ffn_done, SJ * (e - 1))
                sp.dma_start(w2_s[u][:, :, :],
                             w2T[bass.ds(e * HID, HID), :].rearrange("(c p) d -> p c d", p=P)).then_inc(w2_in[u], 16)

            table_v = table.rearrange("(t p) d -> p t d", p=TC)
            with sp.Fori(0, NCHUNK) as c:
                sp.wait_ge(zn_ready, CT * (c + 1))
                sp.dma_start(table_v[:, bass.ds(CT * c, CT), E:ROW],
                             zrow[:, bass.ds(CT * c, CT), E:ROW]).then_inc(table_out, 16)
                sp.dma_start(table_v[:, bass.ds(CT * c, CT), ROW:TROW],
                             zrow[:, bass.ds(CT * c, CT), E + P:ROW]).then_inc(table_out, 16)
            sp.wait_ge(av_done, CB * NCHUNK)
            load_expert(0, 0)
            sp.wait_ge(weights_ready, 1)
            sp.dma_start(table_v[:, :, 0:E], zrow[:, :, 0:E]).then_inc(table_out, 16)
            load_expert(1, 1)
            sp.wait_ge(base_ready, NTC)
            sp.dma_start(out[0:NTOK, :].rearrange("(t p) d -> p t d", p=TC), h2[:, :, :]).then_inc(base_out, 16)
            with sp.Fori(1, E // 2) as it:
                load_expert(2 * it, 0)
                load_expert(2 * it + 1, 1)
            sp.wait_ge(pads_out, 16)

        @block.gpsimd
        def _(pool):
            pool.memset(ones[:, :], 1.0).then_inc(ones_set, 1)
            pool.memset(mhalf[:, :], -0.5).then_inc(ones_set, 1)
            pool.memset(zin[0][:, :, :], 0.0).then_inc(ones_set, 1)
            for w in range(2):
                pool.memset(vp[w][:, :, :], 0.0).then_inc(vp_zero, 1)
            pool.wait_ge(ones_set, 3)

            def root_a(it):
                pool.wait_ge(ve_ready, it + 1)
                pool.tensor_tensor(rstd[:, :], ve[:, :], mhalf[:, :], ALU.pow).then_inc(rstd_ready, 1)

            with pool.Fori(0, ROUNDS - 1) as it:
                root_a(it)

            def take_chunk(c, w):
                pool.tensor_copy(xs[w], xnT[:, :, bass.ds(c * CHUNK, CHUNK)]).then_inc(xs_ready, 1)

            pool.wait_ge(xnT_ready, RING)
            take_chunk(0, 0)
            root_a(ROUNDS - 1)
            pool.wait_ge(xnT_ready, NT)
            take_chunk(1, 1)
            pool.wait_ge(w_in, 16 * W_LOADS)
            pool.wait_ge(rows_back, 16)
            with pool.Fori(0, NTC) as t:
                pool.tensor_tensor(h2[:, bass.ds(t, 1), :], h2[:, bass.ds(t, 1), :], lnb_s[0:TC, :].unsqueeze(1),
                                   ALU.add).then_inc(hb_ready, 1)
            pool.wait_ge(hb_ready, NTC)

            def pool_step(s, w):
                project, attend, after = parts_of(s)
                r = s - 2
                if project and after:
                    pool.wait_ge(energy_done, CB * (s - 1))
                    take_chunk(s, w)
                if after:
                    pool.wait_ge(vew_ready, r + 1)
                    pool.tensor_tensor(rstdw[:, :], vew[:, :], mhalf[0:TC, :], ALU.pow).then_inc(rstdw_ready, 1)
                    pool.wait_ge(y1_ready, CT * (r + 1))
                    pool.tensor_tensor(y2[:, :, :], y1[:, :, :],
                                       lnw_s[0:TC, :].unsqueeze(1).broadcast_to([TC, CT, D]),
                                       ALU.mult).then_inc(y2_ready, 1)
                    pool.wait_ge(y2_ready, r + 1)
                    mine = bass.ds(CT * r, CT)
                    pool.tensor_tensor(h2[:, mine, :], h2[:, mine, :], y2[:, :, :], ALU.add).then_inc(h2_ready, 1)
                    pool.wait_ge(ve2_ready, r + 1)
                    pool.tensor_tensor(rstd2[:, :], ve2[:, :], mhalf[0:TC, :], ALU.pow).then_inc(rstd2_ready, 1)
                if after:
                    pool.wait_ge(ve3_ready, r + 1)
                    pool.tensor_tensor(rms[:, bass.ds(CT * r, CT)], ve3[:, :], mhalf[0:TC, :],
                                       ALU.pow).then_inc(rms_ready, 1)

            steps_of(pool, pool_step)

            pool.wait_ge(index_ready, 2)

            def gather(e, u):
                need(pool, z_turned, 4 * (e - 1))
                need(pool, wslot_ready, e - 1)
                pool.tensor_copy(gi[u][:, :], gather_at[:, bass.ds(e * SJ, SJ)]).then_inc(gi_ready, 1)
                index_copied = in_register(pool, e + 1)
                apart(pool)
                pool.wait_ge(gi_ready, index_copied)
                for j in range(SJ):
                    pool.indirect_dma_start(out=zin[u][:, j, :], out_offset=None, in_=table,
                                            in_offset=bass.IndirectOffsetOnAxis(ap=gi[u][:, j:j + 1], axis=0),
                                            bounds_check=NTOK - 1, oob_is_err=True).then_inc(
                                                rows_in[u][j // (SJ // 2)], 16)

            def add_rows(e, u):
                need(pool, added, 16 * SJ * e)
                pool.tensor_copy(si[:, :], add_at[:, bass.ds(e * SJ, SJ)]).then_inc(si_ready, 1)
                index_copied = in_register(pool, e + 1)
                apart(pool)
                pool.wait_ge(si_ready, index_copied)
                for j in range(SJ):
                    rows_written = in_register(pool, SJ * e + j + 1)
                    apart(pool)
                    pool.wait_ge(y_ready, rows_written)
                    pool.indirect_dma_start(out=out, in_=yo[u][:, j, :], in_offset=None,
                                            out_offset=bass.IndirectOffsetOnAxis(ap=si[:, j:j + 1], axis=0),
                                            bounds_check=NTOK + CAP - 1, oob_is_err=True,
                                            compute_op=ALU.add).then_inc(added, 16)

            pool.wait_ge(table_out, 16 * (2 * NCHUNK + 1))
            pool.wait_ge(pads_out, 16)
            gather(0, 0)
            gather(1, 1)
            pool.wait_ge(base_out, 16)
            add_rows(0, 0)
            gather(2, 0)
            add_rows(1, 1)
            gather(3, 1)
            with pool.Fori(2, E // 2) as it:
                add_rows(2 * it - 2, 0)
                gather(2 * it, 0)
                add_rows(2 * it - 1, 1)
                gather(2 * it + 1, 1)
            add_rows(E - 2, 0)
            add_rows(E - 1, 1)
            pool.wait_ge(added, 16 * SJ * E)

        @block.scalar
        def _(act):
            act.wait_ge(c_in, 16)
            act.wait_ge(w_in, 16 * W_LOADS)
            for hh in range(HEADS):
                act.activation(decay[:, hh, :], col("diff", BLK), ACT.Exp,
                               scale=ls_s[:, hh:hh + 1]).then_inc(exp_ready, 1)

            def xnT_out(it):
                for u in range(RING):
                    t = RING * it + u
                    act.wait_ge(xn_turned, t + 1)
                    act.activation(xnT[:, :, bass.ds(t * P, P)],
                                   ps_t[u][0:HALF, 0:2 * P].rearrange("p (f n) -> p f n", f=2),
                                   ACT.Copy).then_inc(xnT_ready, 1)

            with act.Fori(0, ROUNDS - 1) as it:
                xnT_out(it)

            act.wait_ge(vp_zero, 2)

            def act_step(s, w):
                project, attend, after = parts_of(s)
                r = s - 2

                def item(name):
                    before, at = ring(s, w, name)
                    act.wait_ge(ring_full, before + 1)
                    return ps_ring[at]

                def q_out(f):
                    src = item(f"q{f}")
                    for odd in range(2):
                        ins = act.activation(qm[w][f][:, odd, :], src[0:HALF, 0:CHUNK], ACT.Silu,
                                             scale=cst[0:HALF, _C["mask"].start + odd:_C["mask"].start + odd + 1])
                    ins.then_inc(ring_taken, 1)

                def k_out(f):
                    src = item(f"k{f}")
                    if f:
                        act.activation(g1[w][HALF:HALF + G, :], src[HALF:HALF + G, 0:CHUNK],
                                       ACT.Copy).then_inc(g1_ready, 1)
                    act.activation(kT[w][f][:, :], src[0:HALF, 0:CHUNK], ACT.Silu).then_inc(ring_taken, 1)

                def v_out(i):
                    act.activation(vp[i % 2][:, :, :].rearrange("p j (x d) -> p j x d", d=HD)[:, :, 0:4:3, :],
                                   item(f"v{i}")[0:BLK, 0:D].rearrange("p (j x d) -> p j x d", x=2, d=HD),
                                   ACT.Silu).then_inc(ring_taken, 1)

                def gate_out(f):
                    src = item(f"g{f}")
                    if f == 0 and after:
                        act.wait_ge(go_ready, CB * (s - 1))
                    act.activation(gate[w][:, f, :], src[0:HALF, 0:CHUNK], ACT.Tanh,
                                   scale=0.5).then_inc(ring_taken, 1)

                def turned_out(u0, n):
                    act.activation(xfT[:, :, u0:u0 + n, :],
                                   item(f"t{u0}")[0:HALF, 0:n * 2 * TC].rearrange("p (f u n) -> p f u n", f=2, n=TC),
                                   ACT.Copy).then_inc(ring_taken, 1)

                if attend:
                    v_out(1)
                if project:
                    q_out(0)
                if attend:
                    v_out(2)
                if project:
                    q_out(1)
                    k_out(1)
                if attend:
                    v_out(3)
                if project:
                    k_out(0)
                    gate_out(0)
                if after:
                    turned_out(0, 2)
                if project:
                    v_out(0)
                if after:
                    turned_out(2, 1)
                if project:
                    gate_out(1)
                if after:
                    for u in range(CT):
                        act.wait_ge(xf_ready, CT * r + u + 1)
                        act.activation(squares[:, u, :], xf[:, u, :], ACT.Square,
                                       accum_out=ssq[:, u:u + 1]).then_inc(ssq_ready, 1)
                    act.activation(lgT[:, bass.ds(CHUNK * r, CHUNK)], item("lg")[0:E, 0:CHUNK],
                                   ACT.Copy).then_inc(ring_taken, 1)
                    act.wait_ge(rms_ready, r + 1)
                    for u in range(CT):
                        act.activation(zrow[:, bass.ds(CT * r + u, 1), E:ROW].squeeze(1), xf[:, u, :], ACT.Copy,
                                       scale=rms[:, bass.ds(CT * r + u, 1)]).then_inc(zn_ready, 1)

            act_step(0, 0)
            xnT_out(ROUNDS - 1)
            act_step(1, 1)
            with act.Fori(1, NCHUNK // 2) as it:
                act_step(2 * it, 0)
                act_step(2 * it + 1, 1)
            act_step(NCHUNK, 0)
            act_step(NCHUNK + 1, 1)

            act.wait_ge(ex_ready, 1)
            act.activation(probs[:, :, :], ex[:, :, :], ACT.Exp).then_inc(probs_exp, 1)

            def z_hi_out(e, i):
                act.wait_ge(z_turned, 4 * e + i + 1)
                cols = slice(i // 2 * MOV, (i // 2 + 1) * MOV)
                act.activation((zB if i % 2 else zA_hi)[:, cols], ps_z[i % 2][:, 0:MOV], ACT.Copy).then_inc(z_hi, 1)

            def w_hi_out(e, u, i):
                if i == 0:
                    act.wait_ge(we_in[u], 16 * 3 * (half_of(e, u) + 1))
                    need(act, u_done, 8 * e)
                hi, raw, nw = ((wA_hi, wA, nwA), (wB_hi, wB, nwB))[i]
                act.activation(hi[:, :], raw, ACT.Copy, scale=nw[:, bass.ds(e, 1)]).then_inc(w_hi, 1)

            def silus(e):
                for s in range(2 * HC):
                    act.wait_ge(g_done, 8 * e + s + 1)
                    need(act, a_ready, 8 * e + s - 1)
                    act.activation(silu_g[s % 2], ps_g[s % 2][:, 0:MOV], ACT.Silu).then_inc(silu_ready, 1)

            def weigh(e, u, j):
                if j == 0:
                    act.wait_ge(wslot_ready, e + 1)
                    need(act, added, 16 * SJ * (e - 1))
                act.wait_ge(ffn_done, SJ * e + j + 1)
                act.activation(yo[u][:, j, :], ps_y[j % 2][0:SP_, 0:D], ACT.Copy,
                               scale=wslot[u][:, j:j + 1]).then_inc(y_ready, 1)

            def between(e, u):
                z_hi_out(e + 1, 0)
                z_hi_out(e + 1, 1)
                weigh(e, u, 0)
                weigh(e, u, 1)
                z_hi_out(e + 1, 2)
                z_hi_out(e + 1, 3)
                w_hi_out(e + 1, 1 - u, 0)
                weigh(e, u, 2)
                w_hi_out(e + 1, 1 - u, 1)
                for j in range(3, SJ):
                    weigh(e, u, j)
                silus(e + 1)

            w_hi_out(0, 0, 0)
            w_hi_out(0, 0, 1)
            for i in range(4):
                z_hi_out(0, i)
            silus(0)
            between(0, 0)
            with act.Fori(0, E // 2 - 1) as it:
                between(2 * it + 1, 1)
                between(2 * it + 2, 0)
            for j in range(SJ):
                weigh(E - 1, 1, j)

        @block.vector
        def _(dve):
            dve.wait_ge(w_in, 16 * W_LOADS)

            def norm_round(it):
                for u in range(RING):
                    t = RING * it + u
                    dve.wait_ge(embed_done, t + 1)
                    dve.tensor_tensor(h[:, bass.ds(t, 1), :].squeeze(1), ps_h[u][:, 0:D], b_s[:, :],
                                      ALU.add).then_inc(h_ready, 1)
                    apart(dve)
                    dve.wait_ge(h_ready, t + 1)
                    dve.bn_stats(st[u][:, :], h[:, bass.ds(t, 1), :].squeeze(1)).then_inc(st_ready, 1)
                    apart(dve)
                    dve.wait_ge(st_ready, t + 1)
                    dve.bn_aggr(mv[:, u, :], st[u][:, :]).then_inc(mv_ready, 1)
                dve.wait_ge(mv_ready, RING * (it + 1))
                dve.tensor_scalar(ve[:, :], mv[:, :, 1], EPS_LN, None, ALU.add).then_inc(ve_ready, 1)
                dve.wait_ge(rstd_ready, it + 1)
                for u in range(RING):
                    t = RING * it + u
                    need(dve, xn_turned, t - RING + 1)
                    dve.tensor_scalar(xn[u][:, :], h[:, bass.ds(t, 1), :].squeeze(1), mv[:, u, 0:1],
                                      rstd[:, u:u + 1], ALU.subtract, ALU.mult).then_inc(xn_ready, 1)

            norm_round(0)
            with dve.Fori(1, ROUNDS) as it:
                norm_round(it)

            dve.wait_ge(exp_ready, HEADS)
            dve.tensor_tensor(decay[:, :, :], decay[:, :, :],
                              col("keep", BLK).unsqueeze(1).broadcast_to([BLK, HEADS, BLK]),
                              ALU.mult).then_inc(decay_ready, 1)
            dve.tensor_scalar(wo_h[:, :, :], wo_s[:, :, :], 0.5, None, ALU.mult).then_inc(woh_ready, 1)
            dve.wait_ge(decay_ready, 1)
            decay_v = decay[:, :, :].rearrange("p (f j x) n -> p f j (x n)", f=2, j=PAIRS)

            def dve_step(s, w):
                project, attend, after = parts_of(s)
                c, r = s - 1, s - 2

                def mask_out(i):
                    if attend:
                        dve.wait_ge(energy_done, CB * c + i + 1)
                        dve.tensor_tensor(ed, trio[0:BLK, :, 0:4 * BLK].rearrange("p j (f n) -> p f j n", f=2),
                                          decay_v, ALU.mult).then_inc(ed_ready, 1)

                def gate_mul(i):
                    if attend:
                        cols = slice(i * BLK, (i + 1) * BLK)
                        if i == 0:
                            dve.wait_ge(ring_taken, items_before(s, w))
                        dve.wait_ge(av_done, CB * c + i + 1)
                        dve.scalar_tensor_tensor(gos[1 - w][:, :, cols], gate[1 - w][:, :, cols], 1.0,
                                                 ps_o[0:HALF, 0:2 * BLK].rearrange("p (f n) -> p f n", f=2),
                                                 ALU.add, ALU.mult).then_inc(go_ready, 1)

                mask_out(0)
                if after:
                    for u in range(CT):
                        t = CT * r + u
                        apart(dve)
                        dve.wait_ge(wo_done, CT * r + max(u + 1, 2))
                        dve.bn_stats(stw[:, u, :], ps_w[u]).then_inc(stw_ready, 1)
                        stats_there = in_register(dve, t + 1)
                        apart(dve)
                        dve.wait_ge(stw_ready, stats_there)
                        dve.bn_aggr(mvw[:, u, :], stw[:, u, :]).then_inc(mvw_ready, 1)
                    dve.wait_ge(mvw_ready, CT * (r + 1))
                    dve.tensor_scalar(vew[:, :], mvw[:, :, 1], EPS_LN, None, ALU.add).then_inc(vew_ready, 1)
                    dve.wait_ge(rstdw_ready, r + 1)
                    for u in range(CT):
                        dve.tensor_scalar(y1[:, u, :], ps_w[u], mvw[:, u, 0:1], rstdw[:, u:u + 1],
                                          ALU.subtract, ALU.mult).then_inc(y1_ready, 1)
                gate_mul(0)
                mask_out(1)
                if after:
                    for u in range(CT):
                        t = CT * r + u
                        apart(dve)
                        dve.wait_ge(h2_ready, r + 1)
                        dve.bn_stats(sth[:, u, :], h2[:, bass.ds(t, 1), :].squeeze(1)).then_inc(st2_ready, 1)
                        stats_there = in_register(dve, t + 1)
                        apart(dve)
                        dve.wait_ge(st2_ready, stats_there)
                        dve.bn_aggr(mv2[:, u, :], sth[:, u, :]).then_inc(mv2_ready, 1)
                    dve.wait_ge(mv2_ready, CT * (r + 1))
                    dve.tensor_scalar(ve2[:, :], mv2[:, :, 1], EPS_LN, None, ALU.add).then_inc(ve2_ready, 1)
                gate_mul(1)
                mask_out(2)
                if after:
                    dve.wait_ge(rstd2_ready, r + 1)
                    if not isinstance(r, int) or r:
                        need(dve, zn_ready, CT * r)
                    for u in range(CT):
                        dve.tensor_scalar(xf[:, u, :], h2[:, bass.ds(CT * r + u, 1), :].squeeze(1), mv2[:, u, 0:1],
                                          rstd2[:, u:u + 1], ALU.subtract, ALU.mult).then_inc(xf_ready, 1)
                gate_mul(2)
                mask_out(3)
                gate_mul(3)
                if after:
                    dve.wait_ge(ssq_ready, CT * (r + 1))
                    dve.tensor_scalar(ve3[:, :], ssq[:, :], 1.0 / D, EPS_FFN / 4, ALU.mult,
                                      ALU.add).then_inc(ve3_ready, 1)

            steps_of(dve, dve_step)

            links = [0]

            def link(ins):
                links[0] += 1
                ins.then_inc(route_step, 1)
                dve.wait_ge(route_step, links[0])

            def per_expert(a):
                return a.unsqueeze(1).broadcast_to([TC, E, NTC])

            def by_tile(a):
                return a.rearrange("p e t -> p t e")

            def per_tile(name):
                return colt(name).unsqueeze(2).broadcast_to([TC, E, NTC])

            lg = ps_l[0:TC, 0:E * NTC].rearrange("p (t e) -> p e t", e=E)
            dve.wait_ge(lg_turned, 2)
            link(dve.tensor_reduce(top[:, :], by_tile(lg), AX_X, ALU.max))
            dve.tensor_tensor(ex[:, :, :], lg, per_expert(top[:, :]), ALU.subtract).then_inc(ex_ready, 1)
            dve.wait_ge(probs_exp, 1)
            link(dve.tensor_reduce(rank[:, :], by_tile(probs[:, :, :]), AX_X, ALU.add))
            link(dve.reciprocal(top[:, :], rank[:, :]))
            link(dve.tensor_tensor(left[:, :, :], probs[:, :, :], per_expert(top[:, :]), ALU.mult))
            for k in range(2):
                link(dve.tensor_reduce(best[:, k, :], by_tile(left[:, :, :]), AX_X, ALU.max))
                link(dve.tensor_tensor(same[:, :, :], left[:, :, :], per_expert(best[:, k, :]), ALU.is_equal))
                link(dve.tensor_tensor(cnt[:, :, :], same[:, :, :], per_tile("rank"), ALU.mult))
                link(dve.tensor_reduce(rank[:, :], by_tile(cnt[:, :, :]), AX_X, ALU.max))
                link(dve.tensor_tensor(hot[:, k, :, :], cnt[:, :, :], per_expert(rank[:, :]), ALU.is_equal))
                if k == 0:
                    link(dve.scalar_tensor_tensor(left[:, :, :], hot[:, 0, :, :], -4.0, left[:, :, :], ALU.mult,
                                                  ALU.add))
            link(dve.tensor_tensor(cnt[:, :, :], hot[:, 0, :, :], hot[:, 1, :, :], ALU.add))
            link(dve.tensor_tensor_scan(upto[:, :, :].rearrange("p e t -> p (e t)"), colt("reset"),
                                        cnt[:, :, :].rearrange("p e t -> p (e t)"), 0.0, ALU.mult, ALU.add))
            dve.tensor_tensor(upto[:, :, :], upto[:, :, :], cnt[:, :, :], ALU.subtract).then_inc(counts_ready, 1)
            link(dve.tensor_tensor(top[:, :], best[:, 0, :], best[:, 1, :], ALU.add))
            link(dve.reciprocal(cws[:, :], top[:, :]))
            link(dve.tensor_tensor(cw[:, :, :], best[:, :, :], cws[:, :].unsqueeze(1).broadcast_to([TC, 2, NTC]),
                                   ALU.mult))
            for k in range(2):
                link(dve.tensor_tensor(pick[:, k, :, :], hot[:, k, :, :], per_tile("expert"), ALU.mult))
                link(dve.tensor_reduce(exp_of[:, k, :], by_tile(pick[:, k, :, :]), AX_X, ALU.add))
            dve.wait_ge(places_done, 1)
            for k in range(2):
                link(dve.tensor_tensor(pick[:, k, :, :], hot[:, k, :, :],
                                       ps_d[0:TC, 0:E * NTC].rearrange("p (e t) -> p e t", e=E), ALU.mult))
                link(dve.tensor_reduce(pos[:, k, :], by_tile(pick[:, k, :, :]), AX_X, ALU.add))
            link(dve.tensor_scalar(kept[:, :, :], pos[:, :, :], float(CAP), None, ALU.is_lt))
            link(dve.tensor_scalar(jj[:, :, :], pos[:, :, :], float(SP_), None, ALU.is_ge))
            for i in range(2, SJ):
                link(dve.scalar_tensor_tensor(jj[:, :, :], pos[:, :, :], float(i * SP_), jj[:, :, :], ALU.is_ge,
                                              ALU.add))
            link(dve.scalar_tensor_tensor(pl[:, :, :], jj[:, :, :], -float(SP_), pos[:, :, :], ALU.mult, ALU.add))
            link(dve.scalar_tensor_tensor(ej[:, :, :], exp_of[:, :, :], float(SJ), jj[:, :, :], ALU.mult, ALU.add))
            link(dve.tensor_scalar(far[:, :, :], kept[:, :, :], -FAR, FAR, ALU.mult, ALU.add))
            link(dve.tensor_tensor(ej[:, :, :], ej[:, :, :], far[:, :, :], ALU.add))
            for k in range(2):
                mine = slice(k * NTC, (k + 1) * NTC)
                link(dve.tensor_tensor(hot_e[:, mine, 1, :],
                                       colt("slot_ej").unsqueeze(1).broadcast_to([TC, NTC, E * SJ]),
                                       ej[:, k, :].unsqueeze(2).broadcast_to([TC, NTC, E * SJ]), ALU.is_equal))
                link(dve.tensor_scalar(hot_e[:, mine, 0, :], hot_e[:, mine, 1, :], colt("part"), None, ALU.mult))
                link(dve.tensor_tensor(hot_e[:, mine, 1, :], hot_e[:, mine, 1, :],
                                       colt("tile1").unsqueeze(2).broadcast_to([TC, NTC, E * SJ]), ALU.mult))
                dve.tensor_tensor(hot_p[:, mine, :], colt("slot_p").unsqueeze(1).broadcast_to([TC, NTC, SP_]),
                                  pl[:, k, :].unsqueeze(2).broadcast_to([TC, NTC, SP_]),
                                  ALU.is_equal).then_inc(hots_ready, 1)
            link(dve.tensor_tensor(cw[:, :, :], cw[:, :, :], kept[:, :, :], ALU.mult))
            for k in range(2):
                link(dve.tensor_tensor(pick[:, k, :, :], hot[:, k, :, :], per_expert(cw[:, k, :]), ALU.mult))
            dve.tensor_tensor(zrow[:, :, 0:E].rearrange("p t e -> p e t"), pick[:, 0, :, :], pick[:, 1, :, :],
                              ALU.add).then_inc(weights_ready, 1)
            dve.wait_ge(tokens_done, 1)
            link(dve.tensor_copy(tok_of[:, :], ps_s[0:SP_, 0:2 * E * SJ]))
            part_of, tile_of = tok_of[:, 0:E * SJ], tok_of[:, E * SJ:2 * E * SJ]
            link(dve.scalar_tensor_tensor(token[:, :], tile_of, float(TC), part_of, ALU.mult, ALU.add))
            dve.tensor_scalar(gather_at[:, :], token[:, :], -float(TC), 0.0, ALU.add, ALU.max).then_inc(index_ready, 1)
            link(dve.tensor_scalar(empty[:, :], tile_of, 0.0, None, ALU.is_equal))
            link(dve.tensor_tensor(empty[:, :], empty[:, :], col("slot_id", SP_), ALU.mult))
            dve.scalar_tensor_tensor(add_at[:, :], token[:, :], -float(TC), empty[:, :], ALU.add,
                                     ALU.add).then_inc(index_ready, 1)
            link(dve.tensor_tensor(cws[:, :], cw[:, 0, :], cw[:, 1, :], ALU.add))
            link(dve.reciprocal(top[:, :], rms[:, :]))
            link(dve.tensor_tensor(cws[:, :], cws[:, :], top[:, :], ALU.mult))
            def add_base(t):
                dve.scalar_tensor_tensor(h2[:, t, :], zrow[:, t, E:ROW], cws[:, t:t + 1], h2[:, t, :], ALU.mult,
                                         ALU.add).then_inc(base_ready, 1)

            def w_lo_out(e):
                for i, (w, nw, hi, lo) in enumerate(((wA, nwA, wA_hi, wA_lo), (wB, nwB, wB_hi, wB_lo))):
                    n = P if i == 0 else TAIL
                    dve.wait_ge(w_hi, 2 * e + i + 1)
                    dve.scalar_tensor_tensor(lo[0:n, :], w[0:n, :], nw[0:n, bass.ds(e, 1)],
                                             hi[0:n, :].bitcast(F32), ALU.mult, ALU.subtract).then_inc(w_split, 1)

            def z_lo_out(e, u):
                for i in range(4):
                    cols = slice(i // 2 * MOV, (i // 2 + 1) * MOV)
                    dve.wait_ge(z_hi, 4 * e + i + 1)
                    if i % 2:
                        dve.tensor_tensor(zB[TAIL:P, cols], ps_z[1][TAIL:P, 0:MOV],
                                          zB[TAIL:P, cols].bitcast(F32), ALU.subtract).then_inc(z_split, 1)
                    else:
                        dve.tensor_tensor(zA_lo[:, cols], ps_z[0][:, 0:MOV], zA_hi[:, cols].bitcast(F32),
                                          ALU.subtract).then_inc(z_split, 1)
                need(dve, y_ready, SJ * (e - 1))
                dve.tensor_copy(wslot[u][:, :], zin[u][:, :, bass.ds(e, 1)].squeeze(2)).then_inc(wslot_ready, 1)

            def products(e):
                need(dve, ffn_done, SJ * e)
                for s in range(2 * HC):
                    sh, m = s // HC, s % HC
                    dve.wait_ge(silu_ready, 8 * e + s + 1)
                    dve.wait_ge(u_done, 8 * e + s + 1)
                    dve.tensor_tensor(act_h[:, m, sh * MOV:(sh + 1) * MOV], silu_g[s % 2], ps_u[s % 2][:, 0:MOV],
                                      ALU.mult).then_inc(a_ready, 1)
                    if isinstance(e, int) and e == 0:
                        for t in range(s * CT, (s + 1) * CT):
                            add_base(t)

            w_lo_out(0)
            z_lo_out(0, 0)
            products(0)
            z_lo_out(1, 1)
            w_lo_out(1)
            products(1)
            with dve.Fori(1, E // 2) as it:
                for u in range(2):
                    z_lo_out(2 * it + u, u)
                    w_lo_out(2 * it + u)
                    products(2 * it + u)

        @block.tensor
        def _(pe):
            ident = col("ident")

            pe.wait_ge(wT_in, 16)

            def embed(it):
                for u in range(RING):
                    t = RING * it + u
                    pe.wait_ge(x_in[u], 16 * (it + 1))
                    need(pe, h_ready, t - RING + 1)
                    for k in range(KC):
                        mm = pe.matmul(ps_h[u][:, 0:D], xt[u][:, k, :], wT_s[:, k, :], start=(k == 0),
                                       stop=(k == KC - 1))
                    mm.then_inc(embed_done, 1)

            def turn_xn(it):
                for u in range(RING):
                    t = RING * it + u
                    pe.wait_ge(xn_ready, t + 1)
                    need(pe, xnT_ready, t - RING + 1)
                    for f in range(2):
                        mm = pe.transpose(ps_t[u][0:HALF, f * P:(f + 1) * P], xn[u][:, f * HALF:(f + 1) * HALF],
                                          ident)
                    mm.then_inc(xn_turned, 1)

            embed(0)
            embed(1)
            pe.wait_ge(c_in, 16)
            turn_xn(0)
            with pe.Fori(2, ROUNDS) as it:
                embed(it)
                turn_xn(it - 1)

            pe.wait_ge(w_in, 16 * W_LOADS)

            def pe_step(s, w):
                project, attend, after = parts_of(s)
                c, r = s - 1, s - 2
                before_step = items_before(s, w)

                def item(name):
                    before, at = ring(s, w, name)
                    need(pe, ring_taken, before - 1)
                    return ps_ring[at]

                def proj(name, f, M, weights):
                    out_ = item(name)
                    for k in range(2):
                        mm = pe.matmul(out_[0:M, 0:CHUNK], weights(k), xs[w][:, k, :], start=(k == 0), stop=(k == 1))
                    mm.then_inc(ring_full, 1)

                def query(f):
                    if project:
                        if f == 0:
                            pe.wait_ge(xs_ready, s + 1)
                        proj(f"q{f}", f, HALF, lambda k: wq_s[:, k, f * HALF:(f + 1) * HALF])

                def key(f):
                    if project:
                        proj(f"k{f}", f, HALF + f * G, lambda k: wkg_s[:, k, f * HALF:(f + 1) * HALF + f * G])

                def gates(f):
                    if project:
                        out_ = item(f"g{f}")
                        pe.wait_ge(g1_ready, s + 1)
                        pe.matmul(out_[0:HALF, 0:CHUNK], wg2_s[HALF:HALF + G, f * HALF:(f + 1) * HALF],
                                  g1[w][HALF:HALF + G, :], start=True, stop=True).then_inc(ring_full, 1)

                def values(i):
                    at = xs[w] if i == 0 else xs[1 - w]
                    out_ = item(f"v{i}")
                    for k in range(2):
                        mm = pe.matmul(out_[0:BLK, 0:D], at[:, k, i * BLK:(i + 1) * BLK], wv_s[:, k, :],
                                       start=(k == 0), stop=(k == 1))
                    mm.then_inc(ring_full, 1)

                def logits():
                    out_ = item("lg")
                    pe.wait_ge(ring_taken, ring(s, w, "t2")[0] + 1)
                    for f in range(2):
                        mm = pe.matmul(out_[0:E, 0:CHUNK], gw_s[:, f, :], xfT[:, f, :, :].rearrange("p u n -> p (u n)"),
                                       start=(f == 0), stop=(f == 1))
                    mm.then_inc(ring_full, 1)

                def energy(i):
                    n = CB * c + i
                    if i == 0:
                        pe.wait_ge(ring_taken, before_step - SINCE_K)
                    need(pe, ed_ready, n)
                    cols = slice(i * BLK, (i + 1) * BLK)
                    for f in range(2):
                        for j in range(PAIRS):
                            rows_ = slice(32 * j, 32 * j + 32)
                            mm = pe.matmul(trio[0:BLK, j, f * 2 * BLK:(f + 1) * 2 * BLK], kT[1 - w][f][rows_, cols],
                                           qm[1 - w][f][rows_, :, cols], start=True, stop=True)
                    mm.then_inc(energy_done, 1)

                def attention(i):
                    n = CB * c + i
                    pe.wait_ge(ring_taken, ring(s, w, f"v{i}")[0] + 1 if i else before_step - SINCE_V)
                    pe.wait_ge(ed_ready, n + 1)
                    need(pe, go_ready, n)
                    for f in range(2):
                        for odd in range(2):
                            for j in range(PAIRS):
                                mm = pe.matmul(ps_o[32 * j:32 * j + 32, f * BLK:(f + 1) * BLK],
                                               vp[i % 2][:, PAIRS * f + j, 2 * HD * odd:2 * HD * (odd + 1)],
                                               ed[:, f, j, odd * BLK:(odd + 1) * BLK], start=(odd == 0),
                                               stop=(odd == 1))
                    mm.then_inc(av_done, 1)

                def project_out():
                    pe.wait_ge(go_ready, CB * (r + 1))
                    for u in range(CT):
                        for f in range(2):
                            mm = pe.matmul(ps_w[u], gos[w][:, f, u * TC:(u + 1) * TC], wo_h[:, f, :], start=(f == 0),
                                           stop=(f == 1))
                        mm.then_inc(wo_done, 1)

                def turn(u0, n):
                    out_ = item(f"t{u0}")
                    for u in range(u0, u0 + n):
                        pe.wait_ge(xf_ready, CT * r + u + 1)
                        for f in range(2):
                            at = (f * n + u - u0) * TC
                            mm = pe.transpose(out_[0:HALF, at:at + TC], xf[:, u, f * HALF:(f + 1) * HALF],
                                              ident[0:TC, 0:TC])
                    mm.then_inc(ring_full, 1)

                if attend:
                    energy(0)
                if after:
                    project_out()
                if attend:
                    values(1)
                query(0)
                if attend:
                    attention(0)
                    energy(1)
                    values(2)
                query(1)
                key(1)
                if attend:
                    attention(1)
                    energy(2)
                    values(3)
                key(0)
                gates(0)
                if attend:
                    attention(2)
                    energy(3)
                if after:
                    turn(0, 2)
                if project:
                    values(0)
                if after:
                    turn(2, 1)
                gates(1)
                if attend:
                    attention(3)
                if after:
                    logits()

            pe_step(0, 0)
            turn_xn(ROUNDS - 1)
            pe.wait_ge(xnT_ready, NT)
            pe_step(1, 1)
            pe.wait_ge(woh_ready, 1)
            with pe.Fori(1, NCHUNK // 2) as it:
                pe_step(2 * it, 0)
                pe_step(2 * it + 1, 1)
            pe_step(NCHUNK, 0)

            def turn_logits(r0, r1):
                pe.wait_ge(ring_taken, ring(r1 + 1, (r1 + 1) % 2, "lg")[0] + 1)
                for t in range(CT * r0, CT * r1):
                    mm = pe.transpose(ps_l[0:TC, t * E:(t + 1) * E], lgT[:, t * TC:(t + 1) * TC], ident[0:E, 0:E])
                mm.then_inc(lg_turned, 1)

            pe.wait_ge(go_ready, CB * NCHUNK)
            turn_logits(0, NCHUNK - 1)
            pe_step(NCHUNK + 1, 1)
            turn_logits(NCHUNK - 1, NCHUNK)

            pe.wait_ge(counts_ready, 1)
            pe.matmul(ps_d[0:TC, 0:E * NTC], colt("tri")[:, 0:TC], cnt[:, :, :].rearrange("p e t -> p (e t)"), start=True,
                      stop=False)
            pe.matmul(ps_d[0:TC, 0:E * NTC], ones[0:TC, 0:TC], upto[:, :, :].rearrange("p e t -> p (e t)"), start=False,
                      stop=True).then_inc(places_done, 1)
            for i in range(2 * NTC):
                if i % NTC == 0:
                    pe.wait_ge(hots_ready, i // NTC + 1)
                mm = pe.matmul(ps_s[0:SP_, 0:2 * E * SJ], hot_p[:, i, :],
                               hot_e[:, i, :, :].rearrange("p x s -> p (x s)"), start=(i == 0),
                               stop=(i == 2 * NTC - 1))
            mm.then_inc(tokens_done, 1)

            def turn_rows(e, u, half):
                pe.wait_ge(rows_in[u][half], 16 * (SJ // 2) * (half_of(e, u) + 1))
                for i in (2 * half, 2 * half + 1):
                    need(pe, z_split, 4 * e + i - 1)
                    for x in range(SJ // 2):
                        j = half * (SJ // 2) + x
                        if i % 2:
                            src = zin[u][:, j, E + P:TROW]
                        else:
                            src = zin[u][:, j, E:E + P]
                        mm = pe.transpose(ps_z[i % 2][:, x * SP_:(x + 1) * SP_], src, ident[0:SP_, 0:SP_])
                    mm.then_inc(z_turned, 1)

            def hidden(e):
                pe.wait_ge(w_split, 2 * (e + 1))
                pe.wait_ge(z_split, 4 * (e + 1))
                for s in range(2 * HC):
                    sh, m = s // HC, s % HC
                    need(pe, a_ready, 8 * e + s - 1)
                    cols = slice(sh * MOV, (sh + 1) * MOV)
                    for ps, at, done in ((ps_g, m * P, g_done), (ps_u, HID + m * P, u_done)):
                        rows = slice(at, at + P)
                        parts = ((wA_hi[:, rows], zA_hi[:, cols]), (wA_hi[:, rows], zA_lo[:, cols]),
                                 (wA_lo[:, rows], zA_hi[:, cols]), (wB_hi[:, rows], zB[:, cols]),
                                 (wB_lo[:, rows], zB[0:TAIL, cols]))
                        for i, (w, z) in enumerate(parts):
                            mm = pe.matmul(ps[s % 2][:, 0:MOV], w, z, start=(i == 0), stop=(i == len(parts) - 1))
                        mm.then_inc(done, 1)

            def ffn(e, u, j):
                if j == 0:
                    pe.wait_ge(w2_in[u], 16 * (half_of(e, u) + 1))
                    pe.wait_ge(a_ready, 8 * (e + 1))
                need(pe, y_ready, SJ * e + j - 1)
                for c in range(HC):
                    mm = pe.matmul(ps_y[j % 2][0:SP_, 0:D], act_h[:, c, j * SP_:(j + 1) * SP_],
                                   w2_s[u][:, c, :], start=(c == 0), stop=(c == HC - 1))
                mm.then_inc(ffn_done, 1)

            def between(e, u):
                turn_rows(e + 1, 1 - u, 0)
                ffn(e, u, 0)
                ffn(e, u, 1)
                turn_rows(e + 1, 1 - u, 1)
                for j in range(2, SJ):
                    ffn(e, u, j)
                hidden(e + 1)

            turn_rows(0, 0, 0)
            turn_rows(0, 0, 1)
            hidden(0)
            between(0, 0)
            with pe.Fori(0, E // 2 - 1) as it:
                between(2 * it + 1, 1)
                between(2 * it + 2, 0)
            for j in range(SJ):
                ffn(E - 1, 1, j)


_INS = ["xT", "wT", "b", "ls", "wq", "wkg", "wv", "wg2", "wo", "lnw", "lnb", "gwT", "w13T", "w2T", "nwT", "const"]


def laid_out(x, W, b, ls, Wq, Wk, Wv, Wo, Wg1, Wg2, lnw, lnb, gate_w, w13, w2, norm_w):
    a = np.asarray
    patches = a(x).reshape(B_IMG, CH_IN, GRID, PATCH, GRID, PATCH).transpose(0, 2, 4, 3, 5, 1).reshape(NT, P, KC, P)
    return {
        "xT": np.ascontiguousarray(patches.transpose(0, 3, 2, 1)).reshape(NT * P, KC * P),
        "wT": np.ascontiguousarray(a(W).T), "b": a(b), "ls": a(ls), "wq": a(Wq),
        "wkg": np.concatenate([a(Wk), a(Wg1)], 1), "wv": a(Wv), "wg2": a(Wg2), "wo": a(Wo), "lnw": a(lnw),
        "lnb": a(lnb), "gwT": np.ascontiguousarray(a(gate_w).T),
        "w13T": np.ascontiguousarray(a(w13).transpose(0, 2, 1)).reshape(E * D, 2 * HID),
        "w2T": np.ascontiguousarray(a(w2).transpose(0, 2, 1)).reshape(E * HID, D),
        "nwT": np.ascontiguousarray(a(norm_w).T), "const": constants(),
    }


def kernel(**inputs):
    import concourse.bacc as _bacc
    from concourse.bass_utils import run_bass_kernel_spmd as _run

    i = inputs
    nc = _bacc.Bacc("TRN2", target_bir_lowering=False, num_devices=1)
    arrays = laid_out(i["x"], i["L0_tok_W"], i["L0_tok_b"], i["L0_attn_log_slope"], i["L0_attn_Wq"], i["L0_attn_Wk"],
                      i["L0_attn_Wv"], i["L0_attn_Wo"], i["L0_attn_Wg1"], i["L0_attn_Wg2"], i["L0_attn_ln_w"],
                      i["L0_attn_ln_b"], i["L0_ffn_gate_w"], i["L0_ffn_w13"], i["L0_ffn_w2"], i["L0_ffn_norm_w"])
    args = [nc.dram_tensor(n, arrays[n].shape, mybir.dt.from_np(arrays[n].dtype), kind="ExternalInput").ap()
            for n in _INS]
    args.append(nc.dram_tensor("out", (NTOK + CAP, D), F32, kind="ExternalOutput").ap())
    build(nc, *args)
    r = _run(nc, [arrays], core_ids=[0])
    return r.results[0]["out"][0:NTOK].reshape(B_IMG, SEQ, D)
```

```python
from contextlib import ExitStack

import numpy as np
import concourse.bass as bass
from concourse import mybir

F32 = mybir.dt.float32
F32R = mybir.dt.float32r
BF16 = mybir.dt.bfloat16
I32 = mybir.dt.int32
ALU = mybir.AluOpType
ACT = mybir.ActivationFunctionType
AX_X = mybir.AxisListType.X

P = 128
B_IMG, CH_IN, IMG, PATCH = 64, 3, 96, 16
GRID = IMG // PATCH
SEQ = GRID * GRID
NTOK = B_IMG * SEQ
FEAT = PATCH * PATCH * CH_IN
KC = FEAT // P
D = 192
HALF = D // 2
NT = NTOK // P
RING = 3
ROUNDS = NT // RING
HEADS = 12
HD = D // HEADS
G = 16
BLK = 2 * SEQ
CB = 4
CHUNK = CB * BLK
NCHUNK = NTOK // CHUNK
TC = 96
NTC = NTOK // TC
CT = CHUNK // TC
PAIRS = 3
E = 8
HID = 512
HC = HID // P
CAP = 720
SP_ = 120
SJ = CAP // SP_
MOV = CAP // 2
ROW = E + D
TAIL = D - P
TROW = ROW + TAIL
EPS_LN = 1e-5
EPS_FFN = 1e-6
ROUND = float(3 * 2 ** 22)
FAR = 1000.0

_C = {}
_at = 0
for _name, _n in (("ident", P), ("tri", P), ("mask", 2), ("diff", BLK), ("keep", BLK), ("slot_p", SP_),
                  ("slot_at", E * SJ), ("slot_id", E * SJ), ("rank", E), ("reset", E * NTC),
                  ("tile1", NTC), ("part", 1)):
    _C[_name] = slice(_at, _at + _n)
    _at += _n
NCONST = _at


def constants():
    c = np.zeros((P, NCONST), np.float32)
    p = np.arange(P)
    c[:, _C["ident"]] = np.eye(P)
    c[:, _C["tri"]] = p[:, None] < p[None, :]
    c[:, _C["mask"]] = np.stack([p % 32 < 16, p % 32 >= 16], 1)
    m, n = np.arange(BLK)[:, None], np.arange(BLK)[None, :]
    keep = (n >= m) & (n // SEQ == m // SEQ)
    c[:BLK, _C["diff"]] = (n - m) * keep
    c[:BLK, _C["keep"]] = keep
    c[:, _C["slot_p"]] = np.arange(SP_)
    c[:, _C["slot_at"]] = np.arange(E * SJ) - E * SJ
    c[:, _C["slot_id"]] = NTOK + TC + p[:, None] + SP_ * (np.arange(E * SJ) % SJ)[None, :]
    c[:, _C["rank"]] = E - np.arange(E)
    c[:, _C["reset"]] = (np.arange(E * NTC) % NTC) > 0
    c[:, _C["tile1"]] = np.arange(NTC) + 1
    c[:, _C["part"]] = p[:, None]
    return c


def build(nc, xT, wT, b, ls, wq, wkg, wv, wg2, wo, lnw, lnb, gwT, w13T, w2T, nwT, const, out):
    table = nc.dram_tensor("table", [NTOK, TROW], F32).ap()
    rows = nc.dram_tensor("rows", [NTOK, D], F32).ap()
    with ExitStack() as ctx:
        def sb(name, shape, dt=F32):
            return ctx.enter_context(nc.sbuf_tensor(name, shape, dt))

        def sem(name):
            return ctx.enter_context(nc.semaphore(name))

        def need(eng, s, value):
            if not (isinstance(value, int) and value <= 0):
                eng.wait_ge(s, value)

        cst = sb("cst", [P, NCONST])
        wT_s = sb("wT_s", [P, KC, D])
        b_s = sb("b_s", [P, D])
        ls_s = sb("ls_s", [BLK, HEADS])
        wq_s = sb("wq_s", [HALF, 2, D])
        wkg_s = sb("wkg_s", [HALF, 2, D + G])
        wv_s = sb("wv_s", [HALF, 2, D])
        wg2_s = sb("wg2_s", [HALF + G, D])
        wo_s = sb("wo_s", [HALF, 2, D])
        wo_h = sb("wo_h", [HALF, 2, D])
        lnw_s = sb("lnw_s", [P, D])
        lnb_s = sb("lnb_s", [P, D])
        gw_s = sb("gw_s", [HALF, 2, E])
        nwA = sb("nwA", [P, E])
        nwB = sb("nwB", [P, E])
        ones = sb("ones", [P, P])
        mhalf = sb("mhalf", [P, RING])
        ahead = sb("ahead", [1, 3])

        hold0 = sb("hold0", [P, RING * KC * P])
        hold1 = sb("hold1", [P, 2 * NTOK])
        hold2 = sb("hold2", [P, 2 * NTC * SP_ // 2 + 2 * NTC * E * SJ])
        hold3 = sb("hold3", [P, 17 * CHUNK + 2 * TC * 2 * PAIRS])

        xt = [hold0[:, u * KC * P:(u + 1) * KC * P].rearrange("p (k n) -> p k n", k=KC) for u in range(RING)]
        h = hold2[:, 0:NT * D].rearrange("p (t d) -> p t d", d=D)
        xn = [sb(f"xn{u}", [P, D]) for u in range(RING)]
        st = [sb(f"st{u}", [P, 6]) for u in range(RING)]
        mv = sb("mv", [P, RING, 2])
        ve = sb("ve", [P, RING])
        rstd = sb("rstd", [P, RING])
        xnT = hold1[0:HALF, :].rearrange("p (f n) -> p f n", f=2)

        def chunk_place(parts, i, n=1):
            return hold3[0:parts, i * CHUNK:(i + n) * CHUNK]

        xs = [chunk_place(HALF, 2 * w, 2).rearrange("p (f n) -> p f n", f=2) for w in range(2)]
        qm = [[chunk_place(HALF, 4 + 4 * w + 2 * f, 2).rearrange("p (x n) -> p x n", x=2) for f in range(2)]
              for w in range(2)]
        g1 = [chunk_place(HALF + G, 12 + w) for w in range(2)]
        ed = chunk_place(BLK, 14, 3).rearrange("p (f j n) -> p f j n", f=2, j=PAIRS)
        kT = [[sb(f"kT{w}{f}", [HALF, CHUNK]) for f in range(2)] for w in range(2)]
        gate = [sb(f"gate{w}", [HALF, 2, CHUNK]) for w in range(2)]
        gos = [sb(f"gos{w}", [HALF, 2, CHUNK]) for w in range(2)]
        decay = sb("decay", [BLK, HEADS, BLK])
        vp = [sb(f"vp{w}", [BLK, 2 * PAIRS, 4 * HD]) for w in range(2)]

        h2 = sb("h2", [TC, NTC, D])
        y1 = sb("y1", [TC, CT, D])
        y2 = sb("y2", [TC, CT, D])
        squares = sb("squares", [TC, CT, D])
        stw = sb("stw", [TC, CT, 6])
        mvw = sb("mvw", [TC, CT, 2])
        vew = sb("vew", [TC, CT])
        rstdw = sb("rstdw", [TC, CT])
        sth = sb("sth", [TC, CT, 6])
        mv2 = sb("mv2", [TC, CT, 2])
        ve2 = sb("ve2", [TC, CT])
        rstd2 = sb("rstd2", [TC, CT])
        ssq = sb("ssq", [TC, CT])
        ve3 = sb("ve3", [TC, CT])
        rms = sb("rms", [TC, NTC])
        xf = sb("xf", [TC, CT, D])
        xfT = sb("xfT", [HALF, 2, CT, TC])
        lgT = hold2[0:E, NTC * SP_:NTC * SP_ + NTOK]
        zrow = sb("zrow", [TC, NTC, ROW])

        top = sb("top", [TC, NTC])
        ex = sb("ex", [TC, E, NTC])
        probs = sb("probs", [TC, E, NTC])
        left = sb("left", [TC, E, NTC])
        same = sb("same", [TC, E, NTC])
        best = sb("best", [TC, 2, NTC])
        total = sb("total", [TC, NTC])
        rank = sb("rank", [TC, 2, NTC])
        hot = sb("hot", [TC, 2, E, NTC])
        cnt = sb("cnt", [TC, E, NTC])
        upto = sb("upto", [TC, E, NTC])
        pick = sb("pick", [TC, 2, E, NTC])
        pos = sb("pos", [TC, 2, NTC])
        kept = sb("kept", [TC, 2, NTC])
        cw = sb("cw", [TC, 2, NTC])
        cws = sb("cws", [TC, NTC])
        jj = sb("jj", [TC, 2, NTC])
        pl = sb("pl", [TC, 2, NTC])
        ej = sb("ej", [TC, 2, NTC])
        far = sb("far", [TC, 2, NTC])
        hot_p = hold2[0:TC, 0:2 * NTC * SP_ // 2].bitcast(BF16).rearrange("p (c s) -> p c s", s=SP_)
        at = 2 * NTC * SP_ // 2
        hot_e = hold2[0:TC, at:at + 2 * NTC * E * SJ].bitcast(BF16).rearrange("p (c x s) -> p c x s", x=2, s=E * SJ)
        tok_of = sb("tok_of", [SP_, 2 * E * SJ])
        token = sb("token", [SP_, E * SJ])
        empty = sb("empty", [SP_, E * SJ])
        gather_at = sb("gather_at", [SP_, E * SJ], I32)
        add_at = sb("add_at", [SP_, E * SJ], I32)

        act_h = hold1[:, 0:HC * CAP].rearrange("p (c n) -> p c n", c=HC)
        silu_g = [hold1[:, HC * CAP + s * MOV:HC * CAP + (s + 1) * MOV] for s in range(2)]
        wA, wB = (hold3[:, i * 2 * HID:(i + 1) * 2 * HID] for i in range(2))
        wA_hi = sb("wA_hi", [P, 2 * HID], F32R)
        wA_lo = sb("wA_lo", [P, 2 * HID], F32R)
        wB_hi = sb("wB_hi", [P, 2 * HID], F32R)
        wB_lo = sb("wB_lo", [TAIL, 2 * HID], F32R)
        w2_s = [hold3[:, 4 * HID + u * HC * D:4 * HID + (u + 1) * HC * D].rearrange("p (c d) -> p c d", c=HC)
                for u in range(2)]
        at = 4 * HID + 2 * HC * D
        zin = [sb("zin0", [SP_, SJ, TROW]),
               hold3[0:SP_, at:at + SJ * TROW].rearrange("p (j d) -> p j d", j=SJ)]
        zA_hi = sb("zA_hi", [P, CAP], F32R)
        zA_lo = sb("zA_lo", [P, CAP], F32R)
        zB = sb("zB", [P, CAP], F32R)
        wslot = [sb(f"wslot{u}", [SP_, SJ]) for u in range(2)]
        yo = [hold0[0:SP_, u * SJ * D:(u + 1) * SJ * D].rearrange("p (j d) -> p j d", j=SJ) for u in range(2)]
        gi = [sb(f"gi{u}", [SP_, SJ], I32) for u in range(2)]
        si = sb("si", [SP_, SJ], I32)

        bank = [ctx.enter_context(nc.psum_tensor(f"bank{i}", [P, 512], F32)) for i in range(5)]
        trio = ctx.enter_context(nc.psum_tensor("trio", [P, 3, 512], F32))
        ps_h = [bank[2], bank[3], bank[4]]
        ps_t = [trio[:, u, :] for u in range(RING)]
        ps_ring = [bank[0], bank[1]]
        ps_w = [bank[2][0:TC, 0:D], bank[2][0:TC, D:2 * D], bank[3][0:TC, 0:D]]
        ps_o = bank[4]
        ps_l = bank[4]
        ps_d = bank[4]
        ps_s = bank[0]
        ps_z = [bank[0], bank[1]]
        ps_g = [bank[2], bank[3]]
        ps_u = [bank[4], trio[:, 0, :]]
        ps_y = [trio[:, 1, :], trio[:, 2, :]]

        c_in = sem("c_in")
        wT_in = [sem(f"wT_in{i}") for i in range(2)]
        w_in = sem("w_in")
        x_in = [sem(f"x_in{u}") for u in range(RING)]
        pads_out = sem("pads_out")
        ones_set = sem("ones_set")
        embed_done = sem("embed_done")
        h_ready = sem("h_ready")
        st_ready = sem("st_ready")
        mv_ready = sem("mv_ready")
        ve_ready = sem("ve_ready")
        rstd_ready = sem("rstd_ready")
        xn_ready = sem("xn_ready")
        xn_turned = sem("xn_turned")
        xnT_ready = sem("xnT_ready")
        exp_ready = sem("exp_ready")
        decay_ready = sem("decay_ready")
        woh_ready = sem("woh_ready")
        vp_zero = sem("vp_zero")
        rows_out = sem("rows_out")
        rows_back = sem("rows_back")
        xs_ready = sem("xs_ready")
        ring_full = sem("ring_full")
        ring_taken = sem("ring_taken")
        g1_ready = sem("g1_ready")
        energy_done = sem("energy_done")
        ed_ready = sem("ed_ready")
        av_done = sem("av_done")
        go_ready = sem("go_ready")
        hb_ready = sem("hb_ready")
        wo_done = sem("wo_done")
        stw_ready = sem("stw_ready")
        mvw_ready = sem("mvw_ready")
        vew_ready = sem("vew_ready")
        rstdw_ready = sem("rstdw_ready")
        y1_ready = sem("y1_ready")
        y2_ready = sem("y2_ready")
        h2_ready = sem("h2_ready")
        st2_ready = sem("st2_ready")
        mv2_ready = sem("mv2_ready")
        ve2_ready = sem("ve2_ready")
        rstd2_ready = sem("rstd2_ready")
        xf_ready = sem("xf_ready")
        ssq_ready = sem("ssq_ready")
        ve3_ready = sem("ve3_ready")
        rms_ready = sem("rms_ready")
        zn_ready = sem("zn_ready")
        lg_turned = sem("lg_turned")
        ex_ready = sem("ex_ready")
        probs_exp = sem("probs_exp")
        route_step = sem("route_step")
        counts_ready = sem("counts_ready")
        places_done = sem("places_done")
        column_ready = sem("column_ready")
        kept_ready = sem("kept_ready")
        cw_kept = sem("cw_kept")
        tile_made = [sem(f"tile_made{k}") for k in range(2)]
        part_made = sem("part_made")
        hot_p_made = sem("hot_p_made")
        tokens_done = sem("tokens_done")
        index_ready = sem("index_ready")
        weights_ready = sem("weights_ready")
        base_ready = sem("base_ready")
        table_out = sem("table_out")
        base_out = sem("base_out")
        we_in = [sem(f"we_in{u}") for u in range(2)]
        w2_in = [sem(f"w2_in{u}") for u in range(2)]
        rows_in = [[sem(f"rows_in{u}{half}") for half in range(2)] for u in range(2)]
        gi_ready = sem("gi_ready")
        si_ready = sem("si_ready")
        w_hi = sem("w_hi")
        w_split = sem("w_split")
        z_turned = sem("z_turned")
        z_hi = sem("z_hi")
        z_split = sem("z_split")
        wslot_ready = sem("wslot_ready")
        g_done = sem("g_done")
        u_done = sem("u_done")
        silu_ready = sem("silu_ready")
        a_ready = sem("a_ready")
        ffn_done = sem("ffn_done")
        y_ready = sem("y_ready")
        added = sem("added")

        def apart(eng):
            eng.wait_ge(c_in, 16)

        def in_register(eng, value):
            return value if isinstance(value, int) else eng.to_reg(value)

        def times_tile(eng, k):
            mine = slice(k * NTC, (k + 1) * NTC)
            return eng.tensor_tensor(hot_e[:, mine, 1, :], hot_e[:, mine, 0, :],
                                     colt("tile1").unsqueeze(2).broadcast_to([TC, NTC, E * SJ]), ALU.mult)

        def half_of(e, u):
            return (e - u) // 2

        def col(name, rows=P):
            return cst[0:rows, _C[name]]

        def colt(name):
            return col(name, TC)

        W_LOADS = 13

        FULL = ("v1", "v2", "q0", "k1", "v3", "k0", "g0", "q1", "t0", "t2", "v0", "g1", "lg")
        ITEMS = {0: ("q0", "k1", "k0", "g0", "q1", "v0", "g1"),
                 1: ("v1", "q0", "v2", "k1", "v3", "k0", "g0", "v0", "q1", "g1"),
                 NCHUNK: ("v1", "v2", "v3", "t0", "t2", "lg"), NCHUNK + 1: ("t0", "t2", "lg")}
        BEFORE = len(ITEMS[0]) + len(ITEMS[1])

        def ring(s, w, name):
            if isinstance(s, int) and s < 2:
                n = ITEMS[s].index(name) + (len(ITEMS[0]) if s else 0)
                return n, n % 2
            if isinstance(s, int) and s >= NCHUNK:
                n = BEFORE + len(FULL) * (NCHUNK - 2) + ITEMS[s].index(name)
                n += len(ITEMS[NCHUNK]) if s > NCHUNK else 0
                return n, n % 2
            i = FULL.index(name)
            return len(FULL) * (s - 2) + BEFORE + i, (len(FULL) * w + BEFORE + i) % 2

        def items_of(s):
            return ITEMS.get(s, FULL) if isinstance(s, int) else FULL

        def items_before(s, w):
            return ring(s, w, items_of(s)[0])[0]

        SINCE = 1

        def steps_of(eng, step):
            step(0, 0)
            step(1, 1)
            with eng.Fori(1, NCHUNK // 2) as it:
                step(2 * it, 0)
                step(2 * it + 1, 1)
            step(NCHUNK, 0)
            step(NCHUNK + 1, 1)

        def parts_of(s):
            if not isinstance(s, int):
                return True, True, True
            return s < NCHUNK, 1 <= s <= NCHUNK, s >= 2

        block = ctx.enter_context(nc.Block())

        @block.sync
        def _(sp):
            def load_x(it):
                for u in range(RING):
                    t = RING * it + u
                    need(sp, embed_done, t - RING + 1)
                    sp.dma_start(hold0[:, u * KC * P:(u + 1) * KC * P],
                                 xT[bass.ds(t * P, P), :]).then_inc(x_in[u], 16)

            wT_v = wT.rearrange("(k p) d -> p k d", p=P)
            first = slice(0, KC // 2)
            rest = slice(KC // 2, KC)
            sp.dma_start(wT_s[:, first, :], wT_v[:, first, :]).then_inc(wT_in[0], 16)
            sp.dma_start(hold0[:, 0:KC * P], xT[0:P, :]).then_inc(x_in[0], 16)
            sp.dma_start(wT_s[:, rest, :], wT_v[:, rest, :]).then_inc(wT_in[1], 16)
            for u in range(1, RING):
                sp.dma_start(hold0[:, u * KC * P:(u + 1) * KC * P], xT[u * P:(u + 1) * P, :]).then_inc(x_in[u], 16)
            sp.dma_start(cst[:, :], const).then_inc(c_in, 16)
            sp.dma_start(b_s[:, :], b.partition_broadcast(P)).then_inc(w_in, 16)
            sp.dma_start(ls_s[:, :], ls.partition_broadcast(BLK)).then_inc(w_in, 16)
            sp.dma_start(wq_s[:, :, :], wq.rearrange("(f p) d -> p f d", p=HALF)).then_inc(w_in, 16)
            sp.dma_start(wkg_s[:, :, :], wkg.rearrange("(f p) d -> p f d", p=HALF)).then_inc(w_in, 16)
            sp.dma_start(wv_s[:, :, :], wv.rearrange("(f p) d -> p f d", p=HALF)).then_inc(w_in, 16)
            sp.dma_start(wg2_s[HALF:HALF + G, :], wg2).then_inc(w_in, 16)
            sp.dma_start(wo_s[:, :, :], wo.rearrange("(f p) d -> p f d", p=HALF)).then_inc(w_in, 16)
            sp.dma_start(lnw_s[:, :], lnw.partition_broadcast(P)).then_inc(w_in, 16)
            sp.dma_start(lnb_s[:, :], lnb.partition_broadcast(P)).then_inc(w_in, 16)
            sp.dma_start(gw_s[:, :, :], gwT.rearrange("(f p) e -> p f e", p=HALF)).then_inc(w_in, 16)
            sp.dma_start(nwA[:, :], nwT[0:P, :]).then_inc(w_in, 16)
            for f in range(2):
                sp.dma_start(nwB[f * TAIL:(f + 1) * TAIL, :], nwT[P:D, :]).then_inc(w_in, 16)
            rows_v = rows.rearrange("(t p) d -> p t d", p=P)
            with sp.Fori(1, ROUNDS) as it:
                load_x(it)
                sp.wait_ge(h_ready, RING * it)
                sp.dma_start(rows_v[:, bass.ds(RING * it - RING, RING), :],
                             h[:, bass.ds(RING * it - RING, RING), :]).then_inc(rows_out, 16)
            sp.wait_ge(h_ready, NT)
            sp.dma_start(rows_v[:, NT - RING:NT, :], h[:, NT - RING:NT, :]).then_inc(rows_out, 16)
            sp.wait_ge(rows_out, 16 * ROUNDS)
            sp.dma_start(h2[:, :, :], rows.rearrange("(t p) d -> p t d", p=TC)).then_inc(rows_back, 16)
            sp.wait_ge(ones_set, 3)
            sp.dma_start(out[NTOK:NTOK + CAP, :].rearrange("(p j) d -> p j d", j=SJ),
                         zin[0][:, :, 0:D]).then_inc(pads_out, 16)

            def load_expert(e, u):
                need(sp, w_split, 2 * e)
                sp.dma_start(wA[:, :], w13T[bass.ds(e * D, P), :]).then_inc(we_in[u], 16)
                for f in range(2):
                    sp.dma_start(wB[f * TAIL:(f + 1) * TAIL, :],
                                 w13T[bass.ds(e * D + P, TAIL), :]).then_inc(we_in[u], 16)
                need(sp, ffn_done, SJ * (e - 1))
                sp.dma_start(w2_s[u][:, :, :],
                             w2T[bass.ds(e * HID, HID), :].rearrange("(c p) d -> p c d", p=P)).then_inc(w2_in[u], 16)

            table_v = table.rearrange("(t p) d -> p t d", p=TC)
            with sp.Fori(0, NCHUNK) as c:
                sp.wait_ge(zn_ready, CT * (c + 1))
                sp.dma_start(table_v[:, bass.ds(CT * c, CT), E:ROW],
                             zrow[:, bass.ds(CT * c, CT), E:ROW]).then_inc(table_out, 16)
                sp.dma_start(table_v[:, bass.ds(CT * c, CT), ROW:TROW],
                             zrow[:, bass.ds(CT * c, CT), E + P:ROW]).then_inc(table_out, 16)
            sp.wait_ge(av_done, CB * NCHUNK)
            load_expert(0, 0)
            sp.wait_ge(weights_ready, 1)
            sp.dma_start(table_v[:, :, 0:E], zrow[:, :, 0:E]).then_inc(table_out, 16)
            load_expert(1, 1)
            sp.wait_ge(base_ready, NTC)
            sp.dma_start(out[0:NTOK, :].rearrange("(t p) d -> p t d", p=TC), h2[:, :, :]).then_inc(base_out, 16)
            with sp.Fori(1, E // 2) as it:
                load_expert(2 * it, 0)
                load_expert(2 * it + 1, 1)
            sp.wait_ge(pads_out, 16)

        @block.gpsimd
        def _(pool):
            pool.memset(ones[:, :], 1.0).then_inc(ones_set, 1)
            pool.memset(mhalf[:, :], -0.5).then_inc(ones_set, 1)
            pool.memset(zin[0][:, :, :], 0.0).then_inc(ones_set, 1)
            for w in range(2):
                pool.memset(vp[w][:, :, :], 0.0).then_inc(vp_zero, 1)
            pool.wait_ge(ones_set, 3)

            def root_a(it):
                pool.wait_ge(ve_ready, it + 1)
                pool.tensor_tensor(rstd[:, :], ve[:, :], mhalf[:, :], ALU.pow).then_inc(rstd_ready, 1)

            with pool.Fori(0, ROUNDS - 1) as it:
                root_a(it)

            def take_chunk(c, w):
                pool.tensor_copy(xs[w], xnT[:, :, bass.ds(c * CHUNK, CHUNK)]).then_inc(xs_ready, 1)

            pool.wait_ge(xnT_ready, RING)
            take_chunk(0, 0)
            root_a(ROUNDS - 1)
            pool.wait_ge(xnT_ready, NT)
            take_chunk(1, 1)
            pool.wait_ge(w_in, 16 * W_LOADS)
            pool.wait_ge(rows_back, 16)
            with pool.Fori(0, NTC) as t:
                pool.tensor_tensor(h2[:, bass.ds(t, 1), :], h2[:, bass.ds(t, 1), :], lnb_s[0:TC, :].unsqueeze(1),
                                   ALU.add).then_inc(hb_ready, 1)
            pool.wait_ge(hb_ready, NTC)

            def pool_step(s, w):
                project, attend, after = parts_of(s)
                r = s - 2
                if project and after:
                    pool.wait_ge(energy_done, CB * (s - 1))
                    take_chunk(s, w)
                if after:
                    pool.wait_ge(vew_ready, r + 1)
                    pool.tensor_tensor(rstdw[:, :], vew[:, :], mhalf[0:TC, :], ALU.pow).then_inc(rstdw_ready, 1)
                if after and attend:
                    pool.wait_ge(y1_ready, CT * (r + 1))
                    pool.tensor_tensor(y2[:, :, :], y1[:, :, :],
                                       lnw_s[0:TC, :].unsqueeze(1).broadcast_to([TC, CT, D]),
                                       ALU.mult).then_inc(y2_ready, 1)
                    pool.wait_ge(y2_ready, r + 1)
                    mine = bass.ds(CT * r, CT)
                    pool.tensor_tensor(h2[:, mine, :], h2[:, mine, :], y2[:, :, :], ALU.add).then_inc(h2_ready, 1)
                if after:
                    pool.wait_ge(ve2_ready, r + 1)
                    pool.tensor_tensor(rstd2[:, :], ve2[:, :], mhalf[0:TC, :], ALU.pow).then_inc(rstd2_ready, 1)
                if after:
                    pool.wait_ge(ve3_ready, r + 1)
                    pool.tensor_tensor(rms[:, bass.ds(CT * r, CT)], ve3[:, :], mhalf[0:TC, :],
                                       ALU.pow).then_inc(rms_ready, 1)

            steps_of(pool, pool_step)

            pool.wait_ge(column_ready, 1)
            times_tile(pool, 0).then_inc(tile_made[0], 1)
            pool.wait_ge(kept_ready, 1)
            pool.tensor_tensor(cw[:, :, :], cw[:, :, :], kept[:, :, :], ALU.mult).then_inc(cw_kept, 1)
            pool.wait_ge(cw_kept, 1)
            pool.tensor_tensor(pick[:, :, :, :], hot[:, :, :, :],
                               cw[:, :, :].unsqueeze(2).broadcast_to([TC, 2, E, NTC]), ALU.mult).then_inc(cw_kept, 1)
            pool.wait_ge(cw_kept, 2)
            pool.tensor_tensor(zrow[:, :, 0:E].rearrange("p t e -> p e t"), pick[:, 0, :, :], pick[:, 1, :, :],
                               ALU.add).then_inc(weights_ready, 1)

            pool.wait_ge(index_ready, 1)

            def gather(e, u):
                need(pool, z_turned, 4 * (e - 1))
                need(pool, wslot_ready, e - 1)
                pool.tensor_copy(gi[u][:, :], gather_at[:, bass.ds(e * SJ, SJ)]).then_inc(gi_ready, 1)
                index_copied = in_register(pool, e + 1)
                apart(pool)
                pool.wait_ge(gi_ready, index_copied)
                for j in range(SJ):
                    pool.indirect_dma_start(out=zin[u][:, j, :], out_offset=None, in_=table,
                                            in_offset=bass.IndirectOffsetOnAxis(ap=gi[u][:, j:j + 1], axis=0),
                                            bounds_check=NTOK - 1, oob_is_err=True).then_inc(
                                                rows_in[u][j // (SJ // 2)], 16)

            def add_rows(e, u):
                need(pool, added, 16 * SJ * e)
                pool.tensor_copy(si[:, :], add_at[:, bass.ds(e * SJ, SJ)]).then_inc(si_ready, 1)
                index_copied = in_register(pool, e + 1)
                apart(pool)
                pool.wait_ge(si_ready, index_copied)
                for j in range(SJ):
                    rows_written = in_register(pool, SJ * e + j + 1)
                    apart(pool)
                    pool.wait_ge(y_ready, rows_written)
                    pool.indirect_dma_start(out=out, in_=yo[u][:, j, :], in_offset=None,
                                            out_offset=bass.IndirectOffsetOnAxis(ap=si[:, j:j + 1], axis=0),
                                            bounds_check=NTOK + CAP - 1, oob_is_err=True,
                                            compute_op=ALU.add).then_inc(added, 16)

            pool.wait_ge(table_out, 16 * (2 * NCHUNK + 1))
            pool.wait_ge(pads_out, 16)
            gather(0, 0)
            gather(1, 1)
            pool.wait_ge(index_ready, 2)
            pool.wait_ge(base_out, 16)
            add_rows(0, 0)
            gather(2, 0)
            add_rows(1, 1)
            gather(3, 1)
            with pool.Fori(2, E // 2) as it:
                add_rows(2 * it - 2, 0)
                gather(2 * it, 0)
                add_rows(2 * it - 1, 1)
                gather(2 * it + 1, 1)
            add_rows(E - 2, 0)
            add_rows(E - 1, 1)
            pool.wait_ge(added, 16 * SJ * E)

        @block.scalar
        def _(act):
            act.wait_ge(c_in, 16)
            act.wait_ge(w_in, 16 * W_LOADS)
            for hh in range(HEADS):
                act.activation(decay[:, hh, :], col("diff", BLK), ACT.Exp,
                               scale=ls_s[:, hh:hh + 1]).then_inc(exp_ready, 1)

            act.wait_ge(ones_set, 3)
            act.activation(ahead[:, 2:3], ones[0:1, 0:1], ACT.Silu)

            def xnT_out(it):
                for u in range(RING):
                    t = RING * it + u
                    act.wait_ge(xn_turned, t + 1)
                    act.activation(xnT[:, :, bass.ds(t * P, P)],
                                   ps_t[u][0:HALF, 0:2 * P].rearrange("p (f n) -> p f n", f=2),
                                   ACT.Copy).then_inc(xnT_ready, 1)

            with act.Fori(0, ROUNDS - 1) as it:
                xnT_out(it)

            act.wait_ge(vp_zero, 2)

            def act_step(s, w):
                project, attend, after = parts_of(s)
                r = s - 2

                def item(name):
                    before, at = ring(s, w, name)
                    act.wait_ge(ring_full, before + 1)
                    return ps_ring[at]

                def q_out(f):
                    src = item(f"q{f}")
                    for odd in range(2):
                        ins = act.activation(qm[w][f][:, odd, :], src[0:HALF, 0:CHUNK], ACT.Silu,
                                             scale=cst[0:HALF, _C["mask"].start + odd:_C["mask"].start + odd + 1])
                    ins.then_inc(ring_taken, 1)

                def k_out(f):
                    src = item(f"k{f}")
                    if f:
                        act.activation(g1[w][HALF:HALF + G, :], src[HALF:HALF + G, 0:CHUNK],
                                       ACT.Copy).then_inc(g1_ready, 1)
                    act.activation(kT[w][f][:, :], src[0:HALF, 0:CHUNK], ACT.Silu).then_inc(ring_taken, 1)

                def v_out(i):
                    act.activation(vp[i % 2][:, :, :].rearrange("p j (x d) -> p j x d", d=HD)[:, :, 0:4:3, :],
                                   item(f"v{i}")[0:BLK, 0:D].rearrange("p (j x d) -> p j x d", x=2, d=HD),
                                   ACT.Silu).then_inc(ring_taken, 1)

                def gate_out(f):
                    src = item(f"g{f}")
                    if f == 0 and after:
                        act.wait_ge(go_ready, CB * (s - 1))
                    act.activation(gate[w][:, f, :], src[0:HALF, 0:CHUNK], ACT.Tanh,
                                   scale=0.5).then_inc(ring_taken, 1)

                def turned_out(u0, n):
                    act.activation(xfT[:, :, u0:u0 + n, :],
                                   item(f"t{u0}")[0:HALF, 0:n * 2 * TC].rearrange("p (f u n) -> p f u n", f=2, n=TC),
                                   ACT.Copy).then_inc(ring_taken, 1)

                outs = {"q": q_out, "k": k_out, "v": v_out, "g": gate_out}
                for name in items_of(s):
                    if name[0] in outs:
                        outs[name[0]](int(name[1]))
                    elif name[0] == "t":
                        turned_out(int(name[1]), 2 - int(name[1]) // 2)
                    if project and not attend and name == "q1":
                        xnT_out(ROUNDS - 1)
                if after:
                    for u in range(CT):
                        act.wait_ge(xf_ready, CT * r + u + 1)
                        act.activation(squares[:, u, :], xf[:, u, :], ACT.Square,
                                       accum_out=ssq[:, u:u + 1]).then_inc(ssq_ready, 1)
                    if not attend:
                        act.activation(ahead[:, 0:1], ones[0:1, 0:1], ACT.Exp)
                    act.activation(lgT[:, bass.ds(CHUNK * r, CHUNK)], item("lg")[0:E, 0:CHUNK],
                                   ACT.Copy).then_inc(ring_taken, 1)
                    act.wait_ge(rms_ready, r + 1)
                    for u in range(CT):
                        act.activation(zrow[:, bass.ds(CT * r + u, 1), E:ROW].squeeze(1), xf[:, u, :], ACT.Copy,
                                       scale=rms[:, bass.ds(CT * r + u, 1)]).then_inc(zn_ready, 1)

            act_step(0, 0)
            act_step(1, 1)
            with act.Fori(1, NCHUNK // 2) as it:
                act_step(2 * it, 0)
                act_step(2 * it + 1, 1)
            act_step(NCHUNK, 0)
            act_step(NCHUNK + 1, 1)

            act.wait_ge(ex_ready, 1)
            act.activation(probs[:, :, :], ex[:, :, :], ACT.Exp).then_inc(probs_exp, 1)

            def times_part(k):
                act.wait_ge(tile_made[k], 1)
                act.wait_ge(column_ready, k + 1)
                mine = slice(k * NTC, (k + 1) * NTC)
                act.activation(hot_e[:, mine, 0, :], hot_e[:, mine, 0, :], ACT.Copy,
                               scale=colt("part")).then_inc(part_made, 1)

            def z_hi_out(e, i):
                act.wait_ge(z_turned, 4 * e + i + 1)
                cols = slice(i // 2 * MOV, (i // 2 + 1) * MOV)
                act.activation((zB if i % 2 else zA_hi)[:, cols], ps_z[i % 2][:, 0:MOV], ACT.Copy).then_inc(z_hi, 1)

            def w_hi_out(e, u, i):
                if i == 0:
                    act.wait_ge(we_in[u], 16 * 3 * (half_of(e, u) + 1))
                    need(act, u_done, 8 * e)
                hi, raw, nw = ((wA_hi, wA, nwA), (wB_hi, wB, nwB))[i]
                act.activation(hi[:, :], raw, ACT.Copy, scale=nw[:, bass.ds(e, 1)]).then_inc(w_hi, 1)

            def silus(e, s0, s1):
                for s in range(s0, s1):
                    act.wait_ge(g_done, 8 * e + s + 1)
                    need(act, a_ready, 8 * e + s - 1)
                    act.activation(silu_g[s % 2], ps_g[s % 2][:, 0:MOV], ACT.Silu).then_inc(silu_ready, 1)

            def weigh(e, u, j):
                if j == 0:
                    act.wait_ge(wslot_ready, e + 1)
                    need(act, added, 16 * SJ * (e - 1))
                act.wait_ge(ffn_done, SJ * e + j + 1)
                act.activation(yo[u][:, j, :], ps_y[j % 2][0:SP_, 0:D], ACT.Copy,
                               scale=wslot[u][:, j:j + 1]).then_inc(y_ready, 1)

            def between(e, u):
                z_hi_out(e + 1, 0)
                z_hi_out(e + 1, 1)
                weigh(e, u, 0)
                weigh(e, u, 1)
                z_hi_out(e + 1, 2)
                z_hi_out(e + 1, 3)
                w_hi_out(e + 1, 1 - u, 0)
                weigh(e, u, 2)
                w_hi_out(e + 1, 1 - u, 1)
                for j in range(3, SJ):
                    weigh(e, u, j)
                silus(e + 1, 0, 2 * HC)

            w_hi_out(0, 0, 0)
            w_hi_out(0, 0, 1)
            times_part(0)
            times_part(1)
            act.activation(ahead[:, 1:2], ones[0:1, 0:1], ACT.Silu)
            z_hi_out(0, 0)
            z_hi_out(0, 1)
            silus(0, 0, HC // 2)
            z_hi_out(0, 2)
            z_hi_out(0, 3)
            silus(0, HC // 2, 2 * HC)
            between(0, 0)
            with act.Fori(0, E // 2 - 1) as it:
                between(2 * it + 1, 1)
                between(2 * it + 2, 0)
            for j in range(SJ):
                weigh(E - 1, 1, j)

        @block.vector
        def _(dve):
            dve.wait_ge(w_in, 16 * W_LOADS)

            def norm_round(it):
                for u in range(RING):
                    t = RING * it + u
                    dve.wait_ge(embed_done, t + 1)
                    dve.tensor_tensor(h[:, bass.ds(t, 1), :].squeeze(1), ps_h[u][:, 0:D], b_s[:, :],
                                      ALU.add).then_inc(h_ready, 1)
                    apart(dve)
                    dve.wait_ge(h_ready, t + 1)
                    dve.bn_stats(st[u][:, :], h[:, bass.ds(t, 1), :].squeeze(1)).then_inc(st_ready, 1)
                    apart(dve)
                    dve.wait_ge(st_ready, t + 1)
                    dve.bn_aggr(mv[:, u, :], st[u][:, :]).then_inc(mv_ready, 1)
                dve.wait_ge(mv_ready, RING * (it + 1))
                dve.tensor_scalar(ve[:, :], mv[:, :, 1], EPS_LN, None, ALU.add).then_inc(ve_ready, 1)
                dve.wait_ge(rstd_ready, it + 1)
                for u in range(RING):
                    t = RING * it + u
                    need(dve, xn_turned, t - RING + 1)
                    dve.tensor_scalar(xn[u][:, :], h[:, bass.ds(t, 1), :].squeeze(1), mv[:, u, 0:1],
                                      rstd[:, u:u + 1], ALU.subtract, ALU.mult).then_inc(xn_ready, 1)

            norm_round(0)
            with dve.Fori(1, ROUNDS) as it:
                norm_round(it)

            dve.wait_ge(exp_ready, HEADS)
            dve.tensor_tensor(decay[:, :, :], decay[:, :, :],
                              col("keep", BLK).unsqueeze(1).broadcast_to([BLK, HEADS, BLK]),
                              ALU.mult).then_inc(decay_ready, 1)
            dve.tensor_scalar(wo_h[:, :, :], wo_s[:, :, :], 0.5, None, ALU.mult).then_inc(woh_ready, 1)
            dve.wait_ge(decay_ready, 1)
            decay_v = decay[:, :, :].rearrange("p (f j x) n -> p f j (x n)", f=2, j=PAIRS)

            def dve_step(s, w):
                project, attend, after = parts_of(s)
                c, r = s - 1, s - 2

                def mask_out(i):
                    if attend:
                        dve.wait_ge(energy_done, CB * c + i + 1)
                        dve.tensor_tensor(ed, trio[0:BLK, :, 0:4 * BLK].rearrange("p j (f n) -> p f j n", f=2),
                                          decay_v, ALU.mult).then_inc(ed_ready, 1)

                def residual():
                    dve.wait_ge(y1_ready, CT * (r + 1))
                    dve.tensor_tensor(y2[:, :, :], y1[:, :, :],
                                      lnw_s[0:TC, :].unsqueeze(1).broadcast_to([TC, CT, D]),
                                      ALU.mult).then_inc(y2_ready, 1)
                    dve.wait_ge(y2_ready, r + 1)
                    mine = slice(CT * r, CT * (r + 1))
                    dve.tensor_tensor(h2[:, mine, :], h2[:, mine, :], y2[:, :, :], ALU.add).then_inc(h2_ready, 1)

                def gate_mul(i):
                    if attend:
                        cols = slice(i * BLK, (i + 1) * BLK)
                        if i == 0:
                            dve.wait_ge(ring_taken, items_before(s, w))
                        dve.wait_ge(av_done, CB * c + i + 1)
                        dve.scalar_tensor_tensor(gos[1 - w][:, :, cols], gate[1 - w][:, :, cols], 1.0,
                                                 ps_o[0:HALF, 0:2 * BLK].rearrange("p (f n) -> p f n", f=2),
                                                 ALU.add, ALU.mult).then_inc(go_ready, 1)

                mask_out(0)
                if after:
                    for u in range(CT):
                        t = CT * r + u
                        apart(dve)
                        dve.wait_ge(wo_done, CT * r + max(u + 1, 2))
                        dve.bn_stats(stw[:, u, :], ps_w[u]).then_inc(stw_ready, 1)
                    for u in range(CT):
                        t = CT * r + u
                        stats_there = in_register(dve, t + 1)
                        apart(dve)
                        dve.wait_ge(stw_ready, stats_there)
                        dve.bn_aggr(mvw[:, u, :], stw[:, u, :]).then_inc(mvw_ready, 1)
                    dve.wait_ge(mvw_ready, CT * (r + 1))
                    dve.tensor_scalar(vew[:, :], mvw[:, :, 1], EPS_LN, None, ALU.add).then_inc(vew_ready, 1)
                    dve.wait_ge(rstdw_ready, r + 1)
                    for u in range(CT):
                        dve.tensor_scalar(y1[:, u, :], ps_w[u], mvw[:, u, 0:1], rstdw[:, u:u + 1],
                                          ALU.subtract, ALU.mult).then_inc(y1_ready, 1)
                    if not attend:
                        residual()
                gate_mul(0)
                mask_out(1)
                if after:
                    for u in range(CT):
                        t = CT * r + u
                        apart(dve)
                        dve.wait_ge(h2_ready, r + 1)
                        dve.bn_stats(sth[:, u, :], h2[:, bass.ds(t, 1), :].squeeze(1)).then_inc(st2_ready, 1)
                    for u in range(CT):
                        t = CT * r + u
                        stats_there = in_register(dve, t + 1)
                        apart(dve)
                        dve.wait_ge(st2_ready, stats_there)
                        dve.bn_aggr(mv2[:, u, :], sth[:, u, :]).then_inc(mv2_ready, 1)
                    dve.wait_ge(mv2_ready, CT * (r + 1))
                    dve.tensor_scalar(ve2[:, :], mv2[:, :, 1], EPS_LN, None, ALU.add).then_inc(ve2_ready, 1)
                gate_mul(1)
                mask_out(2)
                if after:
                    dve.wait_ge(rstd2_ready, r + 1)
                    if not isinstance(r, int) or r:
                        need(dve, zn_ready, CT * r)
                    for u in range(CT):
                        dve.tensor_scalar(xf[:, u, :], h2[:, bass.ds(CT * r + u, 1), :].squeeze(1), mv2[:, u, 0:1],
                                          rstd2[:, u:u + 1], ALU.subtract, ALU.mult).then_inc(xf_ready, 1)
                gate_mul(2)
                mask_out(3)
                gate_mul(3)
                if after:
                    dve.wait_ge(ssq_ready, CT * (r + 1))
                    dve.tensor_scalar(ve3[:, :], ssq[:, :], 1.0 / D, EPS_FFN / 4, ALU.mult,
                                      ALU.add).then_inc(ve3_ready, 1)

            steps_of(dve, dve_step)

            links = [0]

            def one_hot_places(c0, c1):
                return dve.tensor_tensor(hot_p[:, c0:c1, :],
                                         colt("slot_p").unsqueeze(1).broadcast_to([TC, c1 - c0, SP_]),
                                         pl[:, :, :].rearrange("p k t -> p (k t)")[:, c0:c1].unsqueeze(2)
                                         .broadcast_to([TC, c1 - c0, SP_]), ALU.is_equal)

            def link(ins):
                links[0] += 1
                ins.then_inc(route_step, 1)
                dve.wait_ge(route_step, links[0])

            def per_expert(a):
                return a.unsqueeze(1).broadcast_to([TC, E, NTC])

            def by_tile(a):
                return a.rearrange("p e t -> p t e")

            def per_tile(name):
                return colt(name).unsqueeze(2).broadcast_to([TC, E, NTC])

            lg = ps_l[0:TC, 0:E * NTC].rearrange("p (t e) -> p e t", e=E)
            dve.wait_ge(lg_turned, 2)
            link(dve.tensor_reduce(top[:, :], by_tile(lg), AX_X, ALU.max))
            dve.tensor_tensor(ex[:, :, :], lg, per_expert(top[:, :]), ALU.subtract).then_inc(ex_ready, 1)
            dve.wait_ge(probs_exp, 1)
            link(dve.tensor_reduce(total[:, :], by_tile(probs[:, :, :]), AX_X, ALU.add))
            link(dve.reciprocal(top[:, :], total[:, :]))
            link(dve.tensor_tensor(left[:, :, :], probs[:, :, :], per_expert(top[:, :]), ALU.mult))
            for k in range(2):
                link(dve.tensor_reduce(best[:, k, :], by_tile(left[:, :, :]), AX_X, ALU.max))
                link(dve.tensor_tensor(same[:, :, :], left[:, :, :], per_expert(best[:, k, :]), ALU.is_equal))
                link(dve.tensor_tensor(cnt[:, :, :], same[:, :, :], per_tile("rank"), ALU.mult))
                link(dve.tensor_reduce(rank[:, k, :], by_tile(cnt[:, :, :]), AX_X, ALU.max))
                link(dve.tensor_tensor(hot[:, k, :, :], cnt[:, :, :], per_expert(rank[:, k, :]), ALU.is_equal))
                if k == 0:
                    link(dve.scalar_tensor_tensor(left[:, :, :], hot[:, 0, :, :], -4.0, left[:, :, :], ALU.mult,
                                                  ALU.add))
            link(dve.tensor_tensor(cnt[:, :, :], hot[:, 0, :, :], hot[:, 1, :, :], ALU.add))
            link(dve.tensor_tensor_scan(upto[:, :, :].rearrange("p e t -> p (e t)"), colt("reset"),
                                        cnt[:, :, :].rearrange("p e t -> p (e t)"), 0.0, ALU.mult, ALU.add))
            dve.tensor_tensor(upto[:, :, :], upto[:, :, :], cnt[:, :, :], ALU.subtract).then_inc(counts_ready, 1)
            link(dve.tensor_tensor(top[:, :], best[:, 0, :], best[:, 1, :], ALU.add))
            link(dve.reciprocal(cws[:, :], top[:, :]))
            link(dve.tensor_tensor(cw[:, :, :], best[:, :, :], cws[:, :].unsqueeze(1).broadcast_to([TC, 2, NTC]),
                                   ALU.mult))
            dve.wait_ge(places_done, 1)
            link(dve.tensor_tensor(pick[:, :, :, :], hot[:, :, :, :],
                                   ps_d[0:TC, 0:E * NTC].rearrange("p (e t) -> p e t", e=E).unsqueeze(1)
                                   .broadcast_to([TC, 2, E, NTC]), ALU.mult))
            link(dve.tensor_reduce(pos[:, :, :], pick[:, :, :, :].rearrange("p k e t -> p k t e"), AX_X, ALU.add))
            link(dve.tensor_scalar(jj[:, :, :], pos[:, :, :], 1.0 / SP_, 0.5 / SP_ - 0.5, ALU.mult, ALU.add))
            link(dve.tensor_scalar(jj[:, :, :], jj[:, :, :], ROUND, None, ALU.add))
            link(dve.tensor_scalar(jj[:, :, :], jj[:, :, :], ROUND, None, ALU.subtract))
            dve.tensor_scalar(far[:, :, :], pos[:, :, :], float(CAP), FAR, ALU.is_ge, ALU.mult)
            dve.scalar_tensor_tensor(pl[:, :, :], jj[:, :, :], -float(SP_), pos[:, :, :], ALU.mult, ALU.add)
            link(dve.scalar_tensor_tensor(ej[:, :, :], rank[:, :, :], -float(SJ), jj[:, :, :], ALU.mult, ALU.add))
            link(dve.tensor_tensor(ej[:, :, :], ej[:, :, :], far[:, :, :], ALU.add))
            dve.tensor_scalar(kept[:, :, :], pos[:, :, :], float(CAP), None, ALU.is_lt).then_inc(kept_ready, 1)
            for k in range(2):
                dve.tensor_tensor(hot_e[:, k * NTC:(k + 1) * NTC, 0, :],
                                  colt("slot_at").unsqueeze(1).broadcast_to([TC, NTC, E * SJ]),
                                  ej[:, k, :].unsqueeze(2).broadcast_to([TC, NTC, E * SJ]),
                                  ALU.is_equal).then_inc(column_ready, 1)
            dve.wait_ge(column_ready, 2)
            times_tile(dve, 1).then_inc(tile_made[1], 1)
            one_hot_places(0, NTC).then_inc(hot_p_made, 1)
            one_hot_places(NTC, 3 * NTC // 2).then_inc(hot_p_made, 1)
            one_hot_places(3 * NTC // 2, 2 * NTC).then_inc(hot_p_made, 1)
            dve.wait_ge(tokens_done, 1)
            link(dve.tensor_copy(tok_of[:, :], ps_s[0:SP_, 0:2 * E * SJ]))
            part_of, tile_of = tok_of[:, 0:E * SJ], tok_of[:, E * SJ:2 * E * SJ]
            link(dve.scalar_tensor_tensor(token[:, :], tile_of, float(TC), part_of, ALU.mult, ALU.add))
            dve.tensor_scalar(gather_at[:, :], token[:, :], -float(TC), 0.0, ALU.add, ALU.max).then_inc(index_ready, 1)
            link(dve.tensor_scalar(empty[:, :], tile_of, 0.0, None, ALU.is_equal))
            link(dve.tensor_tensor(empty[:, :], empty[:, :], col("slot_id", SP_), ALU.mult))
            dve.scalar_tensor_tensor(add_at[:, :], token[:, :], -float(TC), empty[:, :], ALU.add,
                                     ALU.add).then_inc(index_ready, 1)
            dve.wait_ge(cw_kept, 1)
            link(dve.tensor_tensor(cws[:, :], cw[:, 0, :], cw[:, 1, :], ALU.add))
            link(dve.reciprocal(top[:, :], rms[:, :]))
            link(dve.tensor_tensor(cws[:, :], cws[:, :], top[:, :], ALU.mult))
            def add_base(t):
                dve.scalar_tensor_tensor(h2[:, t, :], zrow[:, t, E:ROW], cws[:, t:t + 1], h2[:, t, :], ALU.mult,
                                         ALU.add).then_inc(base_ready, 1)

            def w_lo_out(e):
                for i, (w, nw, hi, lo) in enumerate(((wA, nwA, wA_hi, wA_lo), (wB, nwB, wB_hi, wB_lo))):
                    n = P if i == 0 else TAIL
                    dve.wait_ge(w_hi, 2 * e + i + 1)
                    dve.scalar_tensor_tensor(lo[0:n, :], w[0:n, :], nw[0:n, bass.ds(e, 1)],
                                             hi[0:n, :].bitcast(F32), ALU.mult, ALU.subtract).then_inc(w_split, 1)

            def z_lo_out(e, half):
                for i in (2 * half, 2 * half + 1):
                    cols = slice(i // 2 * MOV, (i // 2 + 1) * MOV)
                    dve.wait_ge(z_hi, 4 * e + i + 1)
                    if i % 2:
                        dve.tensor_tensor(zB[TAIL:P, cols], ps_z[1][TAIL:P, 0:MOV],
                                          zB[TAIL:P, cols].bitcast(F32), ALU.subtract).then_inc(z_split, 1)
                    else:
                        dve.tensor_tensor(zA_lo[:, cols], ps_z[0][:, 0:MOV], zA_hi[:, cols].bitcast(F32),
                                          ALU.subtract).then_inc(z_split, 1)

            def slot_weights(e, u):
                need(dve, y_ready, SJ * (e - 1))
                dve.wait_ge(rows_in[u][0], 16 * (SJ // 2) * (half_of(e, u) + 1))
                dve.wait_ge(rows_in[u][1], 16 * (SJ // 2) * (half_of(e, u) + 1))
                dve.tensor_copy(wslot[u][:, :], zin[u][:, :, bass.ds(e, 1)].squeeze(2)).then_inc(wslot_ready, 1)

            def products(e, s0, s1):
                need(dve, ffn_done, SJ * e)
                for s in range(s0, s1):
                    sh, m = s // HC, s % HC
                    dve.wait_ge(silu_ready, 8 * e + s + 1)
                    dve.wait_ge(u_done, 8 * e + s + 1)
                    dve.tensor_tensor(act_h[:, m, sh * MOV:(sh + 1) * MOV], silu_g[s % 2], ps_u[s % 2][:, 0:MOV],
                                      ALU.mult).then_inc(a_ready, 1)
                    if isinstance(e, int) and e == 0:
                        for t in range(s * CT, (s + 1) * CT):
                            add_base(t)

            w_lo_out(0)
            z_lo_out(0, 0)
            products(0, 0, HC // 2)
            z_lo_out(0, 1)
            products(0, HC // 2, 2 * HC)
            slot_weights(0, 0)

            def dve_expert(e, u):
                z_lo_out(e, 0)
                z_lo_out(e, 1)
                slot_weights(e, u)
                w_lo_out(e)
                products(e, 0, 2 * HC)

            dve_expert(1, 1)
            with dve.Fori(1, E // 2) as it:
                dve_expert(2 * it, 0)
                dve_expert(2 * it + 1, 1)

        @block.tensor
        def _(pe):
            ident = col("ident")

            pe.wait_ge(wT_in[0], 16)

            def embed(it):
                for u in range(RING):
                    t = RING * it + u
                    pe.wait_ge(x_in[u], 16 * (it + 1))
                    need(pe, h_ready, t - RING + 1)
                    for k in range(KC):
                        if isinstance(it, int) and (it, u, k) == (0, 0, KC // 2):
                            pe.wait_ge(wT_in[1], 16)
                        mm = pe.matmul(ps_h[u][:, 0:D], xt[u][:, k, :], wT_s[:, k, :], start=(k == 0),
                                       stop=(k == KC - 1))
                    mm.then_inc(embed_done, 1)

            def turn_xn(it):
                for u in range(RING):
                    t = RING * it + u
                    pe.wait_ge(xn_ready, t + 1)
                    need(pe, xnT_ready, t - RING + 1)
                    for f in range(2):
                        mm = pe.transpose(ps_t[u][0:HALF, f * P:(f + 1) * P], xn[u][:, f * HALF:(f + 1) * HALF],
                                          ident)
                    mm.then_inc(xn_turned, 1)

            embed(0)
            embed(1)
            pe.wait_ge(c_in, 16)
            turn_xn(0)
            with pe.Fori(2, ROUNDS) as it:
                embed(it)
                turn_xn(it - 1)

            pe.wait_ge(w_in, 16 * W_LOADS)

            def turn_logits(r0, r1):
                pe.wait_ge(ring_taken, ring(r1 + 1, (r1 + 1) % 2, "lg")[0] + 1)
                for t in range(CT * r0, CT * r1):
                    mm = pe.transpose(ps_l[0:TC, t * E:(t + 1) * E], lgT[:, t * TC:(t + 1) * TC], ident[0:E, 0:E])
                mm.then_inc(lg_turned, 1)

            def pe_step(s, w):
                project, attend, after = parts_of(s)
                c, r = s - 1, s - 2
                before_step = items_before(s, w)

                def item(name):
                    before, at = ring(s, w, name)
                    need(pe, ring_taken, before - 1)
                    return ps_ring[at]

                def proj(name, M, weights):
                    out_ = item(name)
                    for k in range(2):
                        mm = pe.matmul(out_[0:M, 0:CHUNK], weights(k), xs[w][:, k, :], start=(k == 0), stop=(k == 1))
                    mm.then_inc(ring_full, 1)

                def query(f):
                    if project:
                        if f == 0:
                            pe.wait_ge(xs_ready, s + 1)
                        proj(f"q{f}", HALF, lambda k: wq_s[:, k, f * HALF:(f + 1) * HALF])

                def key(f):
                    if project:
                        proj(f"k{f}", HALF + f * G, lambda k: wkg_s[:, k, f * HALF:(f + 1) * HALF + f * G])

                def gates(f):
                    if project:
                        out_ = item(f"g{f}")
                        pe.wait_ge(g1_ready, s + 1)
                        pe.matmul(out_[0:HALF, 0:CHUNK], wg2_s[HALF:HALF + G, f * HALF:(f + 1) * HALF],
                                  g1[w][HALF:HALF + G, :], start=True, stop=True).then_inc(ring_full, 1)

                def values(i):
                    at = xs[w] if i == 0 else xs[1 - w]
                    out_ = item(f"v{i}")
                    for k in range(2):
                        mm = pe.matmul(out_[0:BLK, 0:D], at[:, k, i * BLK:(i + 1) * BLK], wv_s[:, k, :],
                                       start=(k == 0), stop=(k == 1))
                    mm.then_inc(ring_full, 1)

                def logits():
                    out_ = item("lg")
                    pe.wait_ge(ring_taken, ring(s, w, "t2")[0] + 1)
                    for f in range(2):
                        mm = pe.matmul(out_[0:E, 0:CHUNK], gw_s[:, f, :], xfT[:, f, :, :].rearrange("p u n -> p (u n)"),
                                       start=(f == 0), stop=(f == 1))
                    mm.then_inc(ring_full, 1)

                def energy(i):
                    n = CB * c + i
                    if i == 0:
                        pe.wait_ge(ring_taken, before_step - SINCE)
                    need(pe, ed_ready, n)
                    cols = slice(i * BLK, (i + 1) * BLK)
                    for f in range(2):
                        for j in range(PAIRS):
                            rows_ = slice(32 * j, 32 * j + 32)
                            mm = pe.matmul(trio[0:BLK, j, f * 2 * BLK:(f + 1) * 2 * BLK], kT[1 - w][f][rows_, cols],
                                           qm[1 - w][f][rows_, :, cols], start=True, stop=True)
                    mm.then_inc(energy_done, 1)

                def attention(i):
                    n = CB * c + i
                    pe.wait_ge(ring_taken, ring(s, w, f"v{i}")[0] + 1 if i else before_step - SINCE)
                    pe.wait_ge(ed_ready, n + 1)
                    need(pe, go_ready, n)
                    for f in range(2):
                        for odd in range(2):
                            for j in range(PAIRS):
                                mm = pe.matmul(ps_o[32 * j:32 * j + 32, f * BLK:(f + 1) * BLK],
                                               vp[i % 2][:, PAIRS * f + j, 2 * HD * odd:2 * HD * (odd + 1)],
                                               ed[:, f, j, odd * BLK:(odd + 1) * BLK], start=(odd == 0),
                                               stop=(odd == 1))
                    mm.then_inc(av_done, 1)

                def project_out():
                    pe.wait_ge(go_ready, CB * (r + 1))
                    for u in range(CT):
                        for f in range(2):
                            mm = pe.matmul(ps_w[u], gos[w][:, f, u * TC:(u + 1) * TC], wo_h[:, f, :], start=(f == 0),
                                           stop=(f == 1))
                        mm.then_inc(wo_done, 1)

                def turn(u0, n):
                    out_ = item(f"t{u0}")
                    for u in range(u0, u0 + n):
                        pe.wait_ge(xf_ready, CT * r + u + 1)
                        for f in range(2):
                            at = (f * n + u - u0) * TC
                            mm = pe.transpose(out_[0:HALF, at:at + TC], xf[:, u, f * HALF:(f + 1) * HALF],
                                              ident[0:TC, 0:TC])
                    mm.then_inc(ring_full, 1)

                if attend:
                    energy(0)
                if after:
                    project_out()
                if after and not attend:
                    pe.wait_ge(go_ready, CB * NCHUNK)
                    turn_logits(0, NCHUNK - 1)
                if attend:
                    values(1)
                if attend:
                    if not after:
                        query(0)
                    attention(0)
                    energy(1)
                    values(2)
                if after or not attend:
                    query(0)
                key(1)
                if attend:
                    attention(1)
                    energy(2)
                    values(3)
                key(0)
                gates(0)
                if after or not attend:
                    query(1)
                if project and not attend:
                    turn_xn(ROUNDS - 1)
                if attend:
                    attention(2)
                if after:
                    turn(0, 2)
                    turn(2, 1)
                if attend:
                    energy(3)
                if project:
                    values(0)
                if attend and not after:
                    query(1)
                gates(1)
                if after:
                    logits()
                if attend:
                    attention(3)

            pe_step(0, 0)
            pe.wait_ge(xnT_ready, NT)
            pe_step(1, 1)
            pe.wait_ge(woh_ready, 1)
            with pe.Fori(1, NCHUNK // 2) as it:
                pe_step(2 * it, 0)
                pe_step(2 * it + 1, 1)
            pe_step(NCHUNK, 0)

            pe_step(NCHUNK + 1, 1)
            turn_logits(NCHUNK - 1, NCHUNK)

            pe.wait_ge(counts_ready, 1)
            pe.matmul(ps_d[0:TC, 0:E * NTC], colt("tri")[:, 0:TC], cnt[:, :, :].rearrange("p e t -> p (e t)"),
                      start=True, stop=False)
            pe.matmul(ps_d[0:TC, 0:E * NTC], ones[0:TC, 0:TC], upto[:, :, :].rearrange("p e t -> p (e t)"),
                      start=False, stop=True).then_inc(places_done, 1)
            for i in range(2 * NTC):
                if i % NTC == 0:
                    pe.wait_ge(part_made, i // NTC + 1)
                    pe.wait_ge(hot_p_made, i // NTC + 1)
                if i == 3 * NTC // 2:
                    pe.wait_ge(hot_p_made, 3)
                mm = pe.matmul(ps_s[0:SP_, 0:2 * E * SJ], hot_p[:, i, :],
                               hot_e[:, i, :, :].rearrange("p x s -> p (x s)"), start=(i == 0),
                               stop=(i == 2 * NTC - 1))
            mm.then_inc(tokens_done, 1)

            def turn_rows(e, u, half):
                pe.wait_ge(rows_in[u][half], 16 * (SJ // 2) * (half_of(e, u) + 1))
                for i in (2 * half, 2 * half + 1):
                    need(pe, z_split, 4 * e + i - 1)
                    for x in range(SJ // 2):
                        j = half * (SJ // 2) + x
                        if i % 2:
                            src = zin[u][:, j, E + P:TROW]
                        else:
                            src = zin[u][:, j, E:E + P]
                        mm = pe.transpose(ps_z[i % 2][:, x * SP_:(x + 1) * SP_], src, ident[0:SP_, 0:SP_])
                    mm.then_inc(z_turned, 1)

            def hidden(e, s0, s1):
                if s0 == 0:
                    pe.wait_ge(w_split, 2 * (e + 1))
                for s in range(s0, s1):
                    sh, m = s // HC, s % HC
                    if s == s0 or m == 0:
                        pe.wait_ge(z_split, 4 * e + 2 * (sh + 1))
                    need(pe, a_ready, 8 * e + s - 1)
                    cols = slice(sh * MOV, (sh + 1) * MOV)
                    for ps, at, done in ((ps_g, m * P, g_done), (ps_u, HID + m * P, u_done)):
                        rows = slice(at, at + P)
                        parts = ((wA_hi[:, rows], zA_hi[:, cols]), (wA_hi[:, rows], zA_lo[:, cols]),
                                 (wA_lo[:, rows], zA_hi[:, cols]), (wB_hi[:, rows], zB[:, cols]),
                                 (wB_lo[:, rows], zB[0:TAIL, cols]))
                        for i, (w, z) in enumerate(parts):
                            mm = pe.matmul(ps[s % 2][:, 0:MOV], w, z, start=(i == 0), stop=(i == len(parts) - 1))
                        mm.then_inc(done, 1)

            def ffn(e, u, j):
                if j == 0:
                    pe.wait_ge(w2_in[u], 16 * (half_of(e, u) + 1))
                    pe.wait_ge(a_ready, 8 * (e + 1))
                need(pe, y_ready, SJ * e + j - 1)
                for c in range(HC):
                    mm = pe.matmul(ps_y[j % 2][0:SP_, 0:D], act_h[:, c, j * SP_:(j + 1) * SP_],
                                   w2_s[u][:, c, :], start=(c == 0), stop=(c == HC - 1))
                mm.then_inc(ffn_done, 1)

            def between(e, u):
                turn_rows(e + 1, 1 - u, 0)
                ffn(e, u, 0)
                ffn(e, u, 1)
                turn_rows(e + 1, 1 - u, 1)
                for j in range(2, SJ):
                    ffn(e, u, j)
                hidden(e + 1, 0, 2 * HC)

            turn_rows(0, 0, 0)
            hidden(0, 0, HC // 2)
            turn_rows(0, 0, 1)
            hidden(0, HC // 2, 2 * HC)
            between(0, 0)
            with pe.Fori(0, E // 2 - 1) as it:
                between(2 * it + 1, 1)
                between(2 * it + 2, 0)
            for j in range(SJ):
                ffn(E - 1, 1, j)


_INS = ["xT", "wT", "b", "ls", "wq", "wkg", "wv", "wg2", "wo", "lnw", "lnb", "gwT", "w13T", "w2T", "nwT", "const"]


def laid_out(x, W, b, ls, Wq, Wk, Wv, Wo, Wg1, Wg2, lnw, lnb, gate_w, w13, w2, norm_w):
    a = np.asarray
    patches = a(x).reshape(B_IMG, CH_IN, GRID, PATCH, GRID, PATCH).transpose(0, 2, 4, 3, 5, 1).reshape(NT, P, KC, P)
    return {
        "xT": np.ascontiguousarray(patches.transpose(0, 3, 2, 1)).reshape(NT * P, KC * P),
        "wT": np.ascontiguousarray(a(W).T), "b": a(b), "ls": a(ls), "wq": a(Wq),
        "wkg": np.concatenate([a(Wk), a(Wg1)], 1), "wv": a(Wv), "wg2": a(Wg2), "wo": a(Wo), "lnw": a(lnw),
        "lnb": a(lnb), "gwT": np.ascontiguousarray(a(gate_w).T),
        "w13T": np.ascontiguousarray(a(w13).transpose(0, 2, 1)).reshape(E * D, 2 * HID),
        "w2T": np.ascontiguousarray(a(w2).transpose(0, 2, 1)).reshape(E * HID, D),
        "nwT": np.ascontiguousarray(a(norm_w).T), "const": constants(),
    }


def kernel(**inputs):
    import concourse.bacc as _bacc
    from concourse.bass_utils import run_bass_kernel_spmd as _run

    i = inputs
    nc = _bacc.Bacc("TRN2", target_bir_lowering=False, num_devices=1)
    arrays = laid_out(i["x"], i["L0_tok_W"], i["L0_tok_b"], i["L0_attn_log_slope"], i["L0_attn_Wq"], i["L0_attn_Wk"],
                      i["L0_attn_Wv"], i["L0_attn_Wo"], i["L0_attn_Wg1"], i["L0_attn_Wg2"], i["L0_attn_ln_w"],
                      i["L0_attn_ln_b"], i["L0_ffn_gate_w"], i["L0_ffn_w13"], i["L0_ffn_w2"], i["L0_ffn_norm_w"])
    args = [nc.dram_tensor(n, arrays[n].shape, mybir.dt.from_np(arrays[n].dtype), kind="ExternalInput").ap()
            for n in _INS]
    args.append(nc.dram_tensor("out", (NTOK + CAP, D), F32, kind="ExternalOutput").ap())
    build(nc, *args)
    r = _run(nc, [arrays], core_ids=[0])
    return r.results[0]["out"][0:NTOK].reshape(B_IMG, SEQ, D)
```
